# Optimizing a Trainium2 kernel written in Bass

```python
import numpy as np
import jax
import jax.numpy as jnp

def _softmax(x, axis=-1):
    return jax.nn.softmax(x, axis=axis)

def _gelu(x):
    return jax.nn.gelu(x, approximate=True)

def _silu(x):
    return jax.nn.silu(x)

def _sigmoid(x):
    return jax.nn.sigmoid(x)

def _layernorm(x, axis=-1, eps=1e-05):
    m = jnp.mean(x, axis=axis, keepdims=True)
    v = jnp.var(x, axis=axis, keepdims=True)
    return (x - m) / jnp.sqrt(v + eps)

def _scatter_add(tgt, idx, src, axis=0):
    return tgt.at[idx].add(src)

def _segment_sum(src, seg, n):
    return jax.ops.segment_sum(src, seg, n)
kernel_name = 'mk_gnn_preln_d4_gnn_r8_49657e'

def setup_inputs(seed: int=0):
    np.random.seed(seed)
    _w = jnp.asarray

    def _rec_inputs():
        import jax
        import jax.numpy as jnp
        _gk = jax.random.key(seed)
        x = -8.776e-05 + 1 * jax.random.normal(jax.random.fold_in(_gk, 1), (6250, 128), jnp.float32)
        _s = jax.random.randint(jax.random.fold_in(_gk, 2), (100000,), 0, 6250, jnp.int32)
        _d = jax.random.randint(jax.random.fold_in(_gk, 3), (100000,), 0, 6250, jnp.int32)
        _loop = jnp.arange(6250, dtype=jnp.int32)
        src = jnp.concatenate([_s, _d, _loop])
        dst = jnp.concatenate([_d, _s, _loop])
        _o = jnp.argsort(dst, stable=True)
        src = src[_o]
        dst = dst[_o]
        edge_attr_128 = -4.21973e-05 + 0.999841 * jax.random.normal(jax.random.fold_in(_gk, 12), (206250, 128), jnp.float32)
        edge_weight = jax.random.uniform(jax.random.fold_in(_gk, 14), (206250,), jnp.float32, 0.0, 0.999998)
        return (x, src, dst, edge_attr_128, edge_weight)
    x, src, dst, edge_attr_128, edge_weight = _rec_inputs()

    def _L0_gnn_setup():
        import jax, jax.numpy as jnp
        import numpy as np
        N, D, E = (5000, 128, 80000)
        key = jax.random.key(seed)
        ks = jax.random.split(key, 6)
        x = jax.random.normal(ks[0], (N, D), dtype=jnp.float32)
        edge_index = jax.random.randint(ks[1], (2, E), 0, N, dtype=jnp.int64)
        s = 1.0 / np.sqrt(D)
        Wq = jax.random.normal(ks[2], (D, D), dtype=jnp.float32) * s
        Wk = jax.random.normal(ks[3], (D, D), dtype=jnp.float32) * s
        Wv = jax.random.normal(ks[4], (D, D), dtype=jnp.float32) * s
        Wo = jax.random.normal(ks[5], (D, D), dtype=jnp.float32) * s
        return {'x': x, 'Wq': Wq, 'Wk': Wk, 'Wv': Wv, 'Wo': Wo, 'edge_index': edge_index}
    _L0_gnn_all = _L0_gnn_setup()
    _L0_gnn_in = {k: v for k, v in _L0_gnn_all.items() if k in ('Wq', 'Wk', 'Wv', 'Wo')}
    del _L0_gnn_all

    def _L1_gnn_setup():
        import jax, jax.numpy as jnp
        import numpy as np
        N_NODES = 12500
        N_EDGES = 75000
        D = 128
        key = jax.random.key(seed)
        ks = jax.random.split(key, 6)
        node_feat = jax.random.normal(ks[0], (N_NODES, D), dtype=jnp.float32)
        edge_feat = jax.random.normal(ks[1], (N_EDGES, D), dtype=jnp.float32)
        src = jax.random.randint(ks[2], (N_EDGES,), 0, N_NODES, dtype=jnp.int32)
        dst = jax.random.randint(ks[3], (N_EDGES,), 0, N_NODES, dtype=jnp.int32)
        lim = 1.0 / np.sqrt(D)
        W1 = jax.random.uniform(ks[4], (D, D), jnp.float32, -lim, lim)
        b1 = jnp.zeros((D,), jnp.float32)
        W2 = jax.random.uniform(ks[5], (D, D), jnp.float32, -lim, lim)
        b2 = jnp.zeros((D,), jnp.float32)
        return {'node_feat': node_feat, 'edge_feat': edge_feat, 'src': src, 'dst': dst, 'W1': W1, 'b1': b1, 'W2': W2, 'b2': b2}
    _L1_gnn_all = _L1_gnn_setup()
    _L1_gnn_in = {k: v for k, v in _L1_gnn_all.items() if k in ('W1', 'b1', 'W2', 'b2')}
    del _L1_gnn_all

    def _L2_gnn_setup():
        import jax, jax.numpy as jnp
        import numpy as np
        N_NODES = 12500
        IN_DIM = 128
        OUT_DIM = 128
        N_EDGES = 80000
        BN_EPS = 1e-05

        def _batchnorm(h, gamma, beta):
            mean = jnp.mean(h, axis=0)
            var = jnp.mean(jnp.square(h - mean), axis=0)
            return (h - mean) * jax.lax.rsqrt(var + BN_EPS) * gamma + beta
        key = jax.random.key(seed)
        ks = jax.random.split(key, 8)
        x = jax.random.normal(ks[0], (N_NODES, IN_DIM), dtype=jnp.float32)
        edge_index = jax.random.randint(ks[1], (2, N_EDGES), 0, N_NODES, dtype=jnp.int32)
        s1 = 1.0 / np.sqrt(IN_DIM)
        s2 = 1.0 / np.sqrt(OUT_DIM)
        w1 = jax.random.uniform(ks[2], (IN_DIM, OUT_DIM), minval=-s1, maxval=s1, dtype=jnp.float32)
        b1 = jax.random.uniform(ks[3], (OUT_DIM,), minval=-s1, maxval=s1, dtype=jnp.float32)
        w2 = jax.random.uniform(ks[4], (OUT_DIM, OUT_DIM), minval=-s2, maxval=s2, dtype=jnp.float32)
        b2 = jax.random.uniform(ks[5], (OUT_DIM,), minval=-s2, maxval=s2, dtype=jnp.float32)
        gamma1 = jnp.ones((OUT_DIM,), jnp.float32)
        beta1 = jnp.zeros((OUT_DIM,), jnp.float32)
        gamma2 = jnp.ones((OUT_DIM,), jnp.float32)
        beta2 = jnp.zeros((OUT_DIM,), jnp.float32)
        eps = jnp.zeros((1,), jnp.float32)
        return {'x': x, 'edge_index': edge_index, 'eps': eps, 'w1': w1, 'b1': b1, 'gamma1': gamma1, 'beta1': beta1, 'w2': w2, 'b2': b2, 'gamma2': gamma2, 'beta2': beta2}
    _L2_gnn_all = _L2_gnn_setup()
    _L2_gnn_in = {k: v for k, v in _L2_gnn_all.items() if k in ('eps', 'w1', 'b1', 'gamma1', 'beta1', 'w2', 'b2', 'gamma2', 'beta2')}
    del _L2_gnn_all

    def _L3_gnn_setup():
        import jax, jax.numpy as jnp
        import numpy as np
        N_NODES = 1250
        N_EDGES = 80000
        D_FEAT = 128
        key = jax.random.key(seed)
        k1, k2, k3 = jax.random.split(key, 3)
        x = jax.random.normal(k1, (N_NODES, D_FEAT), dtype=jnp.float32)
        edge_index = jax.random.randint(k2, (2, N_EDGES), 0, N_NODES, dtype=jnp.int64)
        edge_weight = jax.random.uniform(k3, (N_EDGES,), dtype=jnp.float32)
        return {'x': x, 'edge_index': edge_index, 'edge_weight': edge_weight}
    _L3_gnn_all = _L3_gnn_setup()
    _L3_gnn_in = {k: v for k, v in _L3_gnn_all.items() if k in ()}
    del _L3_gnn_all
    return {'x': x, 'src': src, 'dst': dst, 'edge_attr_128': edge_attr_128, 'edge_weight': edge_weight, 'L0_gnn_Wq': _L0_gnn_in['Wq'], 'L0_gnn_Wk': _L0_gnn_in['Wk'], 'L0_gnn_Wv': _L0_gnn_in['Wv'], 'L0_gnn_Wo': _L0_gnn_in['Wo'], 'L1_gnn_W1': _L1_gnn_in['W1'], 'L1_gnn_b1': _L1_gnn_in['b1'], 'L1_gnn_W2': _L1_gnn_in['W2'], 'L1_gnn_b2': _L1_gnn_in['b2'], 'L2_gnn_eps': _L2_gnn_in['eps'], 'L2_gnn_w1': _L2_gnn_in['w1'], 'L2_gnn_b1': _L2_gnn_in['b1'], 'L2_gnn_gamma1': _L2_gnn_in['gamma1'], 'L2_gnn_beta1': _L2_gnn_in['beta1'], 'L2_gnn_w2': _L2_gnn_in['w2'], 'L2_gnn_b2': _L2_gnn_in['b2'], 'L2_gnn_gamma2': _L2_gnn_in['gamma2'], 'L2_gnn_beta2': _L2_gnn_in['beta2']}

def reference(x, src, dst, edge_attr_128, edge_weight, L0_gnn_Wq, L0_gnn_Wk, L0_gnn_Wv, L0_gnn_Wo, L1_gnn_W1, L1_gnn_b1, L1_gnn_W2, L1_gnn_b2, L2_gnn_eps, L2_gnn_w1, L2_gnn_b1, L2_gnn_gamma1, L2_gnn_beta1, L2_gnn_w2, L2_gnn_b2, L2_gnn_gamma2, L2_gnn_beta2):
    import jax
    import jax.numpy as jnp

    def _L0_gnn_ref(x, Wq, Wk, Wv, Wo, edge_index):
        import jax, jax.numpy as jnp
        import numpy as np
        N, D, E = (5000, 128, 80000)
        num_nodes, d = x.shape
        scale = d ** (-0.5)
        sender, receiver = (edge_index[0], edge_index[1])
        Q = x @ Wq
        K = x @ Wk
        V = x @ Wv
        e = jnp.sum(Q[receiver] * K[sender], axis=-1) * scale
        m = jax.ops.segment_max(e, receiver, num_segments=num_nodes)
        m = jnp.where(jnp.isfinite(m), m, 0.0)
        w = jnp.exp(e - m[receiver])
        denom = jax.ops.segment_sum(w, receiver, num_segments=num_nodes)
        numer = jax.ops.segment_sum(w[:, None] * V[sender], receiver, num_segments=num_nodes)
        attn = jnp.where(denom[:, None] > 0, numer / jnp.maximum(denom, 1e-30)[:, None], 0.0)
        return x + attn @ Wo

    def _L1_gnn_ref(node_feat, edge_feat, src, dst, W1, b1, W2, b2):
        import jax, jax.numpy as jnp
        import numpy as np
        N_NODES = 12500
        N_EDGES = 75000
        D = 128
        m = node_feat[src] + edge_feat
        neigh = jax.ops.segment_sum(m, dst, num_segments=node_feat.shape[0])
        h = 2.0 * node_feat + neigh
        h = h @ W1 + b1
        h = jnp.where(h > 0, h, 0.01 * h)
        return h @ W2 + b2

    def _L2_gnn_ref(x, edge_index, eps, w1, b1, gamma1, beta1, w2, b2, gamma2, beta2):
        import jax, jax.numpy as jnp
        import numpy as np
        N_NODES = 12500
        IN_DIM = 128
        OUT_DIM = 128
        N_EDGES = 80000
        BN_EPS = 1e-05

        def _batchnorm(h, gamma, beta):
            mean = jnp.mean(h, axis=0)
            var = jnp.mean(jnp.square(h - mean), axis=0)
            return (h - mean) * jax.lax.rsqrt(var + BN_EPS) * gamma + beta
        row, col = (edge_index[0], edge_index[1])
        agg = jax.ops.segment_sum(x[col], row, num_segments=x.shape[0])
        h = (1.0 + eps) * x + agg
        h = jax.nn.relu(_batchnorm(h @ w1 + b1, gamma1, beta1))
        h = jax.nn.relu(_batchnorm(h @ w2 + b2, gamma2, beta2))
        return h

    def _L3_gnn_ref(x, edge_index, edge_weight):
        import jax, jax.numpy as jnp
        import numpy as np
        N_NODES = 1250
        N_EDGES = 80000
        D_FEAT = 128
        src = x[edge_index[0]]
        msg = src * edge_weight[:, None]
        out = jax.ops.segment_sum(msg, edge_index[1], num_segments=x.shape[0])
        return out
    edge_index = jnp.stack([src, dst])
    h = jnp.maximum(_layernorm(x, axis=-1), 0.0)
    x = x + _L0_gnn_ref(h, L0_gnn_Wq, L0_gnn_Wk, L0_gnn_Wv, L0_gnn_Wo, edge_index)
    h = jnp.maximum(_layernorm(x, axis=-1), 0.0)
    x = x + _L1_gnn_ref(h, edge_attr_128, src, dst, L1_gnn_W1, L1_gnn_b1, L1_gnn_W2, L1_gnn_b2)
    h = jnp.maximum(_layernorm(x, axis=-1), 0.0)
    x = x + _L2_gnn_ref(h, edge_index, L2_gnn_eps, L2_gnn_w1, L2_gnn_b1, L2_gnn_gamma1, L2_gnn_beta1, L2_gnn_w2, L2_gnn_b2, L2_gnn_gamma2, L2_gnn_beta2)
    h = jnp.maximum(_layernorm(x, axis=-1), 0.0)
    x = x + _L3_gnn_ref(h, edge_index, edge_weight)
    return x

_drawn_inputs = setup_inputs


def setup_inputs(seed=0):
    import zlib

    import numpy as np

    out = dict(_drawn_inputs(seed))
    spreads = {'L1_gnn_b1': (0.0, 0.8),
     'L1_gnn_b2': (0.0, 0.337),
     'L2_gnn_gamma1': (1.0, 0.6),
     'L2_gnn_beta1': (0.0, 0.8),
     'L2_gnn_gamma2': (1.0, 0.6),
     'L2_gnn_beta2': (0.0, 0.779)}
    factors = {'L0_gnn_Wq': 7.963, 'L0_gnn_Wk': 7.276, 'L2_gnn_b1': 8.0, 'L2_gnn_b2': 8.0}
    for name, (base, spread) in spreads.items():
        noise = np.random.default_rng([zlib.crc32(name.encode()), seed]).standard_normal(out[name].shape)
        drawn = base * np.exp(spread * noise) if base else spread * noise
        out[name] = jnp.asarray(drawn.astype(out[name].dtype))
    for name, factor in factors.items():
        out[name] = (out[name] * factor).astype(out[name].dtype)
    return out
```

```python
import concourse.bass as bass
from concourse import mybir
from contextlib import ExitStack, contextmanager

F32 = mybir.dt.float32
BF16 = mybir.dt.bfloat16
I32 = mybir.dt.int32
ALU = mybir.AluOpType
ACT = mybir.ActivationFunctionType
AX = mybir.AxisListType

P = 128
D = 128
NODES = 6250
EDGES = 206250
TILES = 50
FULL_TILES = NODES // P
TAIL = NODES - FULL_TILES * P
NODES_PAD = TILES * P
CHUNKS = 8
GROUP = P * CHUNKS
GROUPS = -(-EDGES // GROUP)
FULL_GROUPS = EDGES // GROUP
TAIL_EDGES = EDGES - FULL_GROUPS * GROUP
TAIL_PARTS = TAIL_EDGES // CHUNKS
TAIL_REST = TAIL_EDGES - TAIL_PARTS * CHUNKS
WINDOW = 64
WINDOW_END = 6256
MAX_ROUNDS = NODES // WINDOW + 1
SLOTS = 3
TURNS = (GROUPS - 1) // SLOTS
assert 1 + TURNS * SLOTS == GROUPS
USES = [TURNS + 1] + [TURNS] * (SLOTS - 1)
REPLICAS = CHUNKS // 2
FAR = -1e30
FLOOR = -1e29
LN_EPS = 1e-5
BN_EPS = 1e-5


def each_group(eng, rounds, body):
    with eng.Fori(0, rounds) as r:
        body(r, 0, 0, r * GROUPS, r * USES[0], True)
        with eng.Fori(0, TURNS) as i:
            for s in range(SLOTS):
                slot = (s + 1) % SLOTS
                body(r, i * SLOTS + (s + 1), slot, r * GROUPS + i * SLOTS + (s + 1),
                     r * USES[slot] + i + (1 if slot == 0 else 0), False)


class Core:
    pass


@contextmanager
def semaphores(nc, prefix=""):
    taken = []

    def sem(name):
        taken.append(nc.alloc_semaphore(prefix + name))
        return taken[-1]

    yield sem
    nc.clear_and_free_semaphores(taken)
    nc.all_engine_barrier()


def node_rows(table):
    return (table[0:FULL_TILES * P, :].rearrange("(t p) f -> p t f", p=P),
            table[FULL_TILES * P:NODES, :])


def tile_view(buf):
    return buf[:, :].rearrange("p (t f) -> p t f", f=D)


def setup_stage(nc, c, io):
    with semaphores(nc) as sem:
        loaded, tails, stored = sem("loaded"), sem("tails"), sem("stored")
        pads_set, zeros_set, iotas_made = sem("pads_set"), sem("zeros_set"), sem("iotas_made")
        masks_cleared, masks_made = sem("masks_cleared"), sem("masks_made")
        dve_step, turned = sem("setup_dve_step"), sem("setup_turned")
        dst_i = c.temp[:, 0:GROUPS * CHUNKS].bitcast(I32)
        edge_lo = c.temp[:, 2048:2048 + 2 * P]
        edge_hi = c.temp[:, 2304:2304 + 2 * P]
        ends = c.temp[:, 2560:2564]
        top_f = c.temp[:, 2600:2600 + GROUPS]
        table_i = c.temp[:, 3000:3000 + GROUPS].bitcast(I32)
        widest = c.temp[:, 3300:3301]
        widest_i = c.temp[:, 3301:3302].bitcast(I32)
        iota_i = c.temp[:, 3400:3400 + WINDOW].bitcast(I32)
        part_i = c.temp[:, 3500:3501].bitcast(I32)
        shift_f = c.temp[:, 3501:3502]
        ps = c.psum[0]

        with nc.Block() as block:
            @block.sync
            def _(sp):
                pair = lambda a: a[0:FULL_GROUPS * GROUP].rearrange("(g p j) -> p g j", p=P, j=CHUNKS)
                whole = FULL_GROUPS * CHUNKS
                for name, src, dst in (("src", io["src"], c.src_i), ("dst", io["dst"], dst_i),
                                       ("w", io["edge_weight"], c.weight)):
                    sp.dma_start(dst[:, 0:whole].rearrange("p (g j) -> p g j", j=CHUNKS),
                                 pair(src)).then_inc(loaded, 16)
                sp.wait_ge(pads_set, 3)
                for src, dst in ((io["src"], c.src_i), (io["dst"], dst_i), (io["edge_weight"], c.weight)):
                    at = FULL_GROUPS * GROUP
                    mid = at + TAIL_PARTS * CHUNKS
                    sp.dma_start(dst[0:TAIL_PARTS, whole:whole + CHUNKS],
                                 src[at:mid].rearrange("(p j) -> p j", j=CHUNKS)).then_inc(tails, 16)
                    sp.dma_start(dst[TAIL_PARTS:TAIL_PARTS + 1, whole:whole + TAIL_REST],
                                 src[mid:EDGES].rearrange("(p j) -> p j", p=1)).then_inc(tails, 16)
                sp.wait_ge(dve_step, 8)
                sp.dma_start(c.window_table[:, :], table_i[0:MAX_ROUNDS, :]).then_inc(stored, 16)
                sp.wait_ge(stored, 16 * 2)

            @block.scalar
            def _(act):
                full, rest = node_rows(io["x"])
                act.dma_start(tile_view(c.x)[:, 0:FULL_TILES, :], full).then_inc(loaded, 16)
                for k, name in enumerate(c.weight_names):
                    act.dma_start(c.mats[:, k, :], io[name]).then_inc(loaded, 16)
                for k, name in enumerate(c.column_names):
                    act.dma_start(c.cols[:, k:k + 1],
                                  io[name].rearrange("(p o) -> p o", o=1)).then_inc(loaded, 16)
                act.dma_start(c.eps_one[:, :], io["L2_gnn_eps"].rearrange("(a b) -> a b", a=1)).then_inc(loaded, 16)
                act.wait_ge(zeros_set, 1)
                act.dma_start(c.x[0:TAIL, FULL_TILES * D:(FULL_TILES + 1) * D], rest).then_inc(loaded, 16)
                act.wait_ge(zeros_set, 2)
                act.dma_start(c.table[NODES:NODES_PAD, :].rearrange("(p a) f -> p (a f)", a=2),
                              c.zeros2[0:(NODES_PAD - NODES) // 2, :]).then_inc(stored, 16)

            @block.gpsimd
            def _(pool):
                for m in (c.ident, c.before):
                    nc.gpsimd.memset(m[:, :], 0.0).then_inc(masks_cleared, 1)
                nc.gpsimd.memset(c.ones[:, :], 1.0).then_inc(masks_cleared, 1)
                pool.wait_ge(masks_cleared, 3)
                nc.gpsimd.affine_select(out=c.ident[:, :], in_=c.ident[:, :], compare_op=ALU.not_equal, fill=1.0,
                                        base=0, pattern=[[-1, P]], channel_multiplier=1).then_inc(masks_made, 1)
                nc.gpsimd.affine_select(out=c.before[:, :], in_=c.before[:, :], compare_op=ALU.is_ge, fill=1.0,
                                        base=0, pattern=[[1, P]], channel_multiplier=-1).then_inc(masks_made, 1)
                nc.gpsimd.iota(iota_i, [[1, WINDOW]], base=0, channel_multiplier=0).then_inc(iotas_made, 1)
                nc.gpsimd.iota(part_i, [[1, 1]], base=0, channel_multiplier=1).then_inc(iotas_made, 1)

            @block.vector
            def _(dve):
                done = [0]

                def link(ins):
                    done[0] += 1
                    ins.then_inc(dve_step, 1)
                    dve.wait_ge(dve_step, done[0])

                nc.vector.memset(c.x[:, FULL_TILES * D:], 0.0).then_inc(zeros_set, 1)
                nc.vector.memset(c.zeros2[:, :], 0.0).then_inc(zeros_set, 1)
                whole = FULL_GROUPS * CHUNKS
                nc.vector.memset(c.src_i[:, whole:], 0).then_inc(pads_set, 1)
                nc.vector.memset(dst_i[:, whole:], NODES).then_inc(pads_set, 1)
                nc.vector.memset(c.weight[:, whole:], 0.0).then_inc(pads_set, 1)
                nc.vector.memset(edge_lo[:, :], 0.0)
                link(nc.vector.memset(edge_hi[:, :], 0.0))
                dve.wait_ge(loaded, 16 * c.setup_loads)
                dve.wait_ge(tails, 16 * 6)
                link(nc.vector.tensor_copy(c.dst[:, :], dst_i))
                by_group = c.dst[:, :].rearrange("p (g j) -> p g j", j=CHUNKS)
                nc.vector.tensor_reduce(edge_lo[:, 0:GROUPS], by_group, AX.X, ALU.min)
                link(nc.vector.tensor_reduce(edge_hi[:, 0:GROUPS], by_group, AX.X, ALU.max))
                dve.wait_ge(turned, 1)
                for k, op in enumerate((ALU.min, ALU.min, ALU.max, ALU.max)):
                    last = nc.vector.tensor_reduce(ends[:, k:k + 1], ps[:, k * P:(k + 1) * P], AX.X, op)
                link(last)
                dve.wait_ge(turned, 2)
                nc.vector.tensor_copy(c.first[:, :], ps[:, 0:GROUPS])
                link(nc.vector.tensor_copy(top_f, ps[:, 2 * P:2 * P + GROUPS]))
                dve.wait_ge(iotas_made, 2)
                nc.vector.tensor_copy(c.iota0[:, :], iota_i)
                nc.vector.tensor_scalar(c.dump[:, :], part_i, float(NODES), None, ALU.add)
                nc.vector.tensor_scalar(shift_f, part_i, float(WINDOW), None, ALU.mult)
                link(nc.vector.tensor_tensor(top_f, top_f, c.first[:, :], ALU.subtract))
                link(nc.vector.tensor_reduce(widest, top_f, AX.X, ALU.max))
                link(nc.vector.tensor_scalar(table_i, c.first[:, :], shift_f, float(WINDOW_END), ALU.add, ALU.min))
                link(nc.vector.tensor_copy(widest_i, widest))
                link(nc.vector.tensor_scalar(c.rounds_i[:, :], widest_i, 6, None, ALU.arith_shift_right))
                link(nc.vector.tensor_scalar(c.rounds_i[:, :], c.rounds_i[:, :], 1.0, None, ALU.add))

            @block.tensor
            def _(pe):
                pe.wait_ge(masks_made, 2)
                pe.wait_ge(dve_step, 3)
                for k, part in enumerate((edge_lo[:, 0:P], edge_lo[:, P:2 * P], edge_hi[:, 0:P], edge_hi[:, P:2 * P])):
                    last = nc.tensor.transpose(ps[:, k * P:(k + 1) * P], part, c.ident[:, :])
                last.then_inc(turned, 1)
                pe.wait_ge(dve_step, 4)
                for k in range(4):
                    last = nc.tensor.transpose(ps[:, k * P:(k + 1) * P],
                                               ends[:, k:k + 1].to_broadcast([P, P]), c.ident[:, :])
                last.then_inc(turned, 1)


def project_stage(nc, c, name, weight, source, evacuate, columns=NODES_PAD, before=None):
    step = 512
    parts = [(a, min(step, columns - a)) for a in range(0, columns, step)]
    banks = 4
    with semaphores(nc, name + "_") as sem:
        product_ready, product_taken = sem("product_ready"), sem("product_taken")
        with nc.Block() as block:
            @block.tensor
            def _(pe):
                for k, (a, n) in enumerate(parts):
                    if k >= banks:
                        pe.wait_ge(product_taken, k - banks + 1)
                    nc.tensor.matmul(c.psum[k % banks][:, 0:n], weight, source[:, a:a + n],
                                     start=True, stop=True).then_inc(product_ready, 1)

            @block.scalar
            def _(act):
                for k, (a, n) in enumerate(parts):
                    act.wait_ge(product_ready, k + 1)
                    evacuate(slice(a, a + n), c.psum[k % banks][:, 0:n]).then_inc(product_taken, 1)


def turn_stage(nc, c, name, source, take):
    five = 5
    with semaphores(nc, name + "_") as sem:
        turned, taken = sem("turned"), sem("taken")
        with nc.Block() as block:
            @block.tensor
            def _(pe):
                for k in range(TILES // five):
                    if k >= 2:
                        pe.wait_ge(taken, k - 1)
                    for q in range(five):
                        a = (k * five + q) * P
                        last = nc.tensor.transpose(c.psum_wide[k % 2][:, q * P:(q + 1) * P], source[:, a:a + P],
                                                   c.ident[:, :])
                    last.then_inc(turned, 1)

            @block.vector
            def _(dve):
                for k in range(TILES // five):
                    dve.wait_ge(turned, k + 1)
                    take(slice(k * five * P, (k + 1) * five * P), c.psum_wide[k % 2][:, 0:five * P]).then_inc(taken, 1)


def normalise_stage(nc, c, name, keep_x=False):
    parts = 5
    width = TILES // parts
    with semaphores(nc, name + "_") as sem:
        summed, scaled, centred, squared, spread = (sem("summed"), sem("scaled"), sem("centred"), sem("squared"), sem("spread"))
        rooted, inverted, normal, stored = sem("rooted"), sem("inverted"), sem("normal"), sem("stored")
        x3, h3, q3 = tile_view(c.x), tile_view(c.rows2), tile_view(c.rows1)
        with nc.Block() as block:
            @block.vector
            def _(dve):
                nc.vector.tensor_reduce(c.stat_a[:, :], x3, AX.X, ALU.add).then_inc(summed, 1)
                dve.wait_ge(summed, 1)
                nc.vector.tensor_scalar(c.stat_a[:, :], c.stat_a[:, :], 1.0 / D, None, ALU.mult).then_inc(scaled, 1)
                dve.wait_ge(scaled, 1)
                for k in range(parts):
                    t = slice(k * width, (k + 1) * width)
                    nc.vector.tensor_tensor(h3[:, t, :], x3[:, t, :],
                                            c.stat_a[:, t].unsqueeze(2).to_broadcast([P, width, D]),
                                            ALU.subtract).then_inc(centred, 1)
                for k in range(parts):
                    t = slice(k * width, (k + 1) * width)
                    dve.wait_ge(squared, k + 1)
                    nc.vector.tensor_reduce(c.stat_b[:, t], q3[:, t, :], AX.X, ALU.add).then_inc(spread, 1)
                dve.wait_ge(rooted, 1)
                nc.vector.reciprocal(c.stat_b[:, :], c.stat_a[:, :]).then_inc(inverted, 1)
                dve.wait_ge(inverted, 1)
                for k in range(parts):
                    t = slice(k * width, (k + 1) * width)
                    nc.vector.scalar_tensor_tensor(out=h3[:, t, :], in0=h3[:, t, :], scalar=0.0,
                                                   in1=c.stat_b[:, t].unsqueeze(2).to_broadcast([P, width, D]),
                                                   op0=ALU.max, op1=ALU.mult).then_inc(normal, 1)

            @block.scalar
            def _(act):
                for k in range(parts):
                    act.wait_ge(centred, k + 1)
                    w = slice(k * width * D, (k + 1) * width * D)
                    nc.scalar.activation(c.rows1[:, w], c.rows2[:, w], ACT.Square).then_inc(squared, 1)
                act.wait_ge(spread, parts)
                nc.scalar.activation(c.stat_a[:, :], c.stat_b[:, :], ACT.Sqrt, scale=1.0 / D,
                                     bias=c.eps_col[:, :]).then_inc(rooted, 1)

            @block.sync
            def _(sp):
                sp.wait_ge(normal, parts)
                full, rest = node_rows(c.table)
                sp.dma_start(full, h3[:, 0:FULL_TILES, :]).then_inc(stored, 16)
                sp.dma_start(rest, h3[0:TAIL, FULL_TILES, :]).then_inc(stored, 16)
                if keep_x:
                    sp.dma_start(c.x_store[:, :], c.x[:, :]).then_inc(stored, 16)
                sp.wait_ge(stored, 48 if keep_x else 32)


def windows_program(sp, c, rounds_done, windows_loaded, r):
    sp.wait_ge(rounds_done, r + 1)
    sp.dma_start(c.window[:, :], c.window_table[bass.ds(r, 1), :]).then_inc(windows_loaded, 16)


def attention_stage(nc, c):
    gt, h_sum = c.x, c.pair
    with semaphores(nc, "a_") as sem:
        rounds_done, windows_loaded, gate = sem("rounds_done"), sem("windows_loaded"), c.gate
        idx_loaded = [sem(f"idx_loaded{s}") for s in range(SLOTS)]
        rows_gathered = [sem(f"rows_gathered{s}") for s in range(SLOTS)]
        half_turned, half_copied, weights_summed = sem("half_turned"), sem("half_copied"), sem("weights_summed")
        rows_turned, turned_copied, scores_ready = sem("rows_turned"), sem("turned_copied"), sem("scores_ready")
        mismatch_ready, masked, chunks_maxed = sem("mismatch_ready"), sem("masked"), sem("chunks_maxed")
        maxima_turned, maxima_found, maxima_spread = sem("maxima_turned"), sem("maxima_found"), sem("maxima_spread")
        maxima_new, maxima_step, maxima_kept, shifted = sem("maxima_new"), sem("maxima_step"), sem("maxima_kept"), sem("shifted")
        weights_ready, weighted, rescaled, added = sem("weights_ready"), sem("weighted"), sem("rescaled"), sem("added")
        replicas_cleared, cleared, iota_moved = sem("replicas_cleared"), sem("cleared"), sem("iota_moved")
        psT, psS, psM, psV = c.psum_wide[0], c.psum[4], c.psum[5], c.psum[6]
        mism, B, W = c.onehot[:, 0:512], c.onehot[:, 512:1024], c.onehot[:, 1024:1536]
        B3 = B.rearrange("p (j w) -> p j w", w=WINDOW)
        W3 = W.rearrange("p (j w) -> p j w", w=WINDOW)
        S3 = psS[:, :].rearrange("p (j w) -> p j w", w=WINDOW)
        small = c.small
        bm, mnew, mg = small[:, 0:P], small[:, P:P + WINDOW], small[:, 192:193]
        mstep = [small[:, 256 + 64 * s:320 + 64 * s] for s in range(SLOTS)]
        wsum = c.onehot[:, 512 * SLOTS:512 * SLOTS + WINDOW]
        mscale = [small[:, 448 + 64 * s:512 + 64 * s] for s in range(SLOTS)]
        with nc.Block() as block:
            @block.sync
            def _(sp):
                rounds = sp.value_load(c.rounds_i[0:1, 0:1], min_val=1, max_val=MAX_ROUNDS)

                def body(r, g, slot, t, use, first):
                    if first:
                        windows_program(sp, c, rounds_done, windows_loaded, r)
                    sp.wait_ge(rows_turned, t + 1)
                    sp.dma_start(c.idx[:, slot, :], c.src_i[:, bass.ds(g * CHUNKS, CHUNKS)]).then_inc(idx_loaded[slot], 16)
                each_group(sp, rounds, body)

            @block.gpsimd
            def _(pool):
                rounds = pool.value_load(c.rounds_i[0:1, 0:1], min_val=1, max_val=MAX_ROUNDS)

                def body(r, g, slot, t, use, first):
                    pool.wait_ge(idx_loaded[slot], use * 16 + 16)
                    pool.wait_ge(weighted, t + 1)
                    pool.sem_inc(gate, 1)
                    for j in range(CHUNKS):
                        nc.gpsimd.indirect_dma_start(
                            c.rows[:, slot, j, :], None, c.table[:, :],
                            bass.IndirectOffsetOnAxis(ap=c.idx[:, slot, j:j + 1], axis=0)).then_inc(rows_gathered[slot], 16)
                each_group(pool, rounds, body)

            @block.tensor
            def _(pe):
                pe.sem_inc(weighted, SLOTS)
                pe.sem_inc(scores_ready, 1)
                pe.sem_inc(rows_turned, SLOTS)
                rounds = pe.value_load(c.rounds_i[0:1, 0:1], min_val=1, max_val=MAX_ROUNDS)

                def weigh(slot, t):
                    pe.wait_ge(weights_ready, t + 1)
                    pe.wait_ge(added, t + 1)
                    for j in range(CHUNKS):
                        nc.tensor.matmul(psV[:, 0:WINDOW], c.rows[:, slot, j, :], W3[:, j, :],
                                         start=(j == 0), stop=(j == CHUNKS - 1))
                    pe.wait_ge(weights_summed, t + 1)
                    nc.tensor.matmul(psV[:, WINDOW:2 * WINDOW], c.ones[:, :], wsum,
                                     start=True, stop=True).then_inc(weighted, 1)

                def body(r, g, slot, t, use, first):
                    if first:
                        pe.wait_ge(windows_loaded, r * 16 + 16)
                        pe.sem_inc(gate, 1)
                    pe.wait_ge(rows_gathered[slot], use * (16 * CHUNKS) + 16 * CHUNKS)
                    pe.wait_ge(turned_copied, t + 1)
                    for half, turned in enumerate((half_turned, rows_turned)):
                        for j in range(half * CHUNKS // 2, (half + 1) * CHUNKS // 2):
                            last = nc.tensor.transpose(psT[:, j * P:(j + 1) * P], c.rows[:, slot, j, :], c.ident[:, :])
                        last.then_inc(turned, 1)
                    base = pe.value_load(c.window[0:1, bass.ds(g, 1)], min_val=0, max_val=WINDOW_END)
                    pe.wait_ge(half_copied, t + 1)
                    pe.wait_ge(masked, t + 1)
                    for j in range(CHUNKS):
                        if j == CHUNKS // 2:
                            pe.wait_ge(turned_copied, t + 2)
                        last = nc.tensor.matmul(psS[:, j * WINDOW:(j + 1) * WINDOW], c.turned[:, j * P:(j + 1) * P],
                                                gt[:, bass.ds(base, WINDOW)], start=True, stop=True)
                    last.then_inc(scores_ready, 1)
                    if not first:
                        weigh((slot + SLOTS - 1) % SLOTS, t - 1)
                    pe.wait_ge(chunks_maxed, t + 1)
                    nc.tensor.transpose(psM[:, 0:P], bm, c.ident[:, :]).then_inc(maxima_turned, 1)
                    pe.wait_ge(maxima_found, t + 1)
                    nc.tensor.transpose(psM[:, P:2 * P], mg.to_broadcast([P, P]), c.ident[:, :]).then_inc(maxima_spread, 1)

                with pe.Fori(0, rounds) as r:
                    body(r, 0, 0, r * GROUPS, r * USES[0], True)
                    with pe.Fori(0, TURNS) as i:
                        for s in range(SLOTS):
                            slot = (s + 1) % SLOTS
                            body(r, i * SLOTS + (s + 1), slot, r * GROUPS + i * SLOTS + (s + 1),
                                 r * USES[slot] + i + (1 if slot == 0 else 0), False)
                    weigh((GROUPS - 1) % SLOTS, r * GROUPS + (GROUPS - 1))

            @block.scalar
            def _(act):
                act.sem_inc(turned_copied, 1)
                for rep in c.replicas:
                    act.dma_start(rep[:, :].rearrange("(t p) f -> p t f", p=P),
                                  c.zeros[:, :].unsqueeze(1).to_broadcast([P, TILES, D])).then_inc(replicas_cleared, 16)
                rounds = act.value_load(c.rounds_i[0:1, 0:1], min_val=1, max_val=MAX_ROUNDS)

                def body(r, g, slot, t, use, first):
                    mid = CHUNKS * P // 2
                    act.wait_ge(half_turned, t + 1)
                    act.wait_ge(scores_ready, t + 1)
                    nc.scalar.activation(c.turned[:, 0:mid], psT[:, 0:mid], ACT.Copy).then_inc(half_copied, 1)
                    act.wait_ge(rows_turned, t + 1 + SLOTS)
                    nc.scalar.activation(c.turned[:, mid:], psT[:, mid:], ACT.Copy).then_inc(turned_copied, 1)
                    act.wait_ge(shifted, t + 1)
                    nc.scalar.activation(mscale[slot], mstep[slot], ACT.Exp)
                    act.wait_ge(weighted, t + SLOTS)
                    nc.scalar.activation(W, B, ACT.Exp).then_inc(weights_ready, 1)
                each_group(act, rounds, body)
                act.wait_ge(replicas_cleared, 16 * REPLICAS)

            @block.vector
            def _(dve):
                dve.sem_inc(masked, 1)
                dve.sem_inc(added, 1)
                nc.vector.memset(c.pair[:, :], 0.0).then_inc(cleared, 1)
                nc.vector.memset(c.maxima[:, :], FLOOR).then_inc(cleared, 1)
                nc.vector.tensor_copy(c.iota[:, :], c.iota0[:, :]).then_inc(cleared, 1)
                nc.vector.memset(bm, FLOOR).then_inc(cleared, 1)
                dve.wait_ge(cleared, 4)
                dve.sem_inc(rounds_done, 1)
                rounds = dve.value_load(c.rounds_i[0:1, 0:1], min_val=1, max_val=MAX_ROUNDS)
                both = c.pair[:, :].rearrange("p (k n) -> p k n", k=2)

                def sum_weights(t):
                    dve.wait_ge(weights_ready, t + 1)
                    nc.vector.tensor_reduce(wsum, W.rearrange("p (j w) -> p w j", w=WINDOW), AX.X,
                                            ALU.add).then_inc(weights_summed, 1)

                def add(g, slot, t):
                    base = dve.value_load(c.window[0:1, bass.ds(g, 1)], min_val=0, max_val=WINDOW_END)
                    dve.wait_ge(weights_ready, t + 1)
                    nc.vector.tensor_tensor(both[:, :, bass.ds(base, WINDOW)], both[:, :, bass.ds(base, WINDOW)],
                                            mscale[slot].unsqueeze(1).to_broadcast([P, 2, WINDOW]),
                                            ALU.mult).then_inc(rescaled, 1)
                    dve.wait_ge(rescaled, t + 1)
                    dve.wait_ge(weighted, t + 1 + SLOTS)
                    nc.vector.tensor_tensor(both[:, :, bass.ds(base, WINDOW)], both[:, :, bass.ds(base, WINDOW)],
                                            psV[:, 0:2 * WINDOW].rearrange("p (k w) -> p k w", k=2),
                                            ALU.add).then_inc(added, 1)

                def body(r, g, slot, t, use, first):
                    if first:
                        dve.wait_ge(windows_loaded, r * 16 + 16)
                        dve.sem_inc(gate, 1)
                    nc.vector.scalar_tensor_tensor(
                        out=mism.rearrange("p (j w) -> p j w", w=WINDOW),
                        in0=c.iota[:, :].unsqueeze(1).to_broadcast([P, CHUNKS, WINDOW]),
                        scalar=c.first[:, bass.ds(g, 1)],
                        in1=c.dst[:, bass.ds(g * CHUNKS, CHUNKS)].unsqueeze(2).to_broadcast([P, CHUNKS, WINDOW]),
                        op0=ALU.add, op1=ALU.not_equal).then_inc(mismatch_ready, 1)
                    if not first:
                        sum_weights(t - 1)
                    dve.wait_ge(mismatch_ready, t + 1)
                    dve.wait_ge(scores_ready, t + 2)
                    nc.vector.scalar_tensor_tensor(out=B, in0=mism, scalar=FAR, in1=psS[:, :],
                                                   op0=ALU.mult, op1=ALU.add).then_inc(masked, 1)
                    dve.wait_ge(masked, t + 2)
                    nc.vector.tensor_reduce(bm[:, 0:WINDOW], B.rearrange("p (j w) -> p w j", w=WINDOW), AX.X,
                                            ALU.max).then_inc(chunks_maxed, 1)
                    base = dve.value_load(c.window[0:1, bass.ds(g, 1)], min_val=0, max_val=WINDOW_END)
                    dve.wait_ge(maxima_turned, t + 1)
                    nc.vector.tensor_reduce(mg, psM[:, 0:P], AX.X, ALU.max).then_inc(maxima_found, 1)
                    dve.wait_ge(maxima_spread, t + 1)
                    nc.vector.tensor_tensor(mnew, c.maxima[:, bass.ds(base, WINDOW)], psM[:, P:P + WINDOW],
                                            ALU.max).then_inc(maxima_new, 1)
                    dve.wait_ge(maxima_new, t + 1)
                    nc.vector.tensor_tensor(mstep[slot], c.maxima[:, bass.ds(base, WINDOW)], mnew,
                                            ALU.subtract).then_inc(maxima_step, 1)
                    nc.vector.tensor_tensor(B3, B3, mnew.unsqueeze(1).to_broadcast([P, CHUNKS, WINDOW]),
                                            ALU.subtract).then_inc(shifted, 1)
                    dve.wait_ge(maxima_step, t + 1)
                    nc.vector.tensor_tensor(c.maxima[:, bass.ds(base, WINDOW)], mnew, mnew,
                                            ALU.max).then_inc(maxima_kept, 1)
                    dve.wait_ge(maxima_kept, t + 1)
                    dve.sem_inc(gate, 1)
                    if not first:
                        add(g - 1, (slot + SLOTS - 1) % SLOTS, t - 1)
                        dve.wait_ge(added, t + 1)
                        dve.sem_inc(gate, 1)

                with dve.Fori(0, rounds) as r:
                    body(r, 0, 0, r * GROUPS, r * USES[0], True)
                    with dve.Fori(0, TURNS) as i:
                        for s in range(SLOTS):
                            slot = (s + 1) % SLOTS
                            body(r, i * SLOTS + (s + 1), slot, r * GROUPS + i * SLOTS + (s + 1),
                                 r * USES[slot] + i + (1 if slot == 0 else 0), False)
                    sum_weights(r * GROUPS + (GROUPS - 1))
                    add(GROUPS - 1, (GROUPS - 1) % SLOTS, r * GROUPS + (GROUPS - 1))
                    nc.vector.tensor_scalar(c.iota[:, :], c.iota[:, :], float(WINDOW), None, ALU.add).then_inc(iota_moved, 1)
                    dve.wait_ge(iota_moved, r + 1)
                    dve.wait_ge(added, r * GROUPS + (GROUPS + 1))
                    dve.sem_inc(rounds_done, 1)


def sum_stage(nc, c, name, acc, edge_features=None, weighted_edges=False):
    with semaphores(nc, name + "_") as sem:
        rounds_done, windows_loaded, gate = sem("rounds_done"), sem("windows_loaded"), c.gate
        idx_loaded = [sem(f"idx_loaded{s}") for s in range(SLOTS)]
        rows_gathered = [sem(f"rows_gathered{s}") for s in range(SLOTS)]
        features_loaded = [sem(f"features_loaded{s}") for s in range(SLOTS)]
        match_ready, onehot_ready, messages_ready = sem("match_ready"), sem("onehot_ready"), sem("messages_ready")
        summed, added, iota_reset, iota_moved = sem("summed"), sem("added"), sem("iota_reset"), sem("iota_moved")
        ps = [c.psum[s] for s in range(SLOTS)]
        hot = [c.onehot[:, s * 512:(s + 1) * 512].rearrange("p (j w) -> p j w", w=WINDOW) for s in range(SLOTS)]
        rows_seen = summed if edge_features is None else messages_ready
        with nc.Block() as block:
            @block.sync
            def _(sp):
                rounds = sp.value_load(c.rounds_i[0:1, 0:1], min_val=1, max_val=MAX_ROUNDS)

                def body(r, g, slot, t, use, first):
                    if first:
                        windows_program(sp, c, rounds_done, windows_loaded, r)
                    sp.wait_ge(rows_seen, t + 1)
                    sp.dma_start(c.idx[:, slot, :], c.src_i[:, bass.ds(g * CHUNKS, CHUNKS)]).then_inc(idx_loaded[slot], 16)
                each_group(sp, rounds, body)

            if edge_features is not None:
                @block.scalar
                def _(act):
                    rounds = act.value_load(c.rounds_i[0:1, 0:1], min_val=1, max_val=MAX_ROUNDS)

                    def load(g, slot, t, last):
                        act.wait_ge(messages_ready, t + 1)
                        if not last:
                            act.dma_start(c.features[:, slot, :, :],
                                          edge_features[bass.ds(g * GROUP, GROUP), :].rearrange("(p j) f -> p j f", j=CHUNKS)
                                          ).then_inc(features_loaded[slot], 16)
                            return
                        at, mid = FULL_GROUPS * GROUP, FULL_GROUPS * GROUP + TAIL_PARTS * CHUNKS
                        act.dma_start(c.features[0:TAIL_PARTS, slot, :, :],
                                      edge_features[at:mid, :].rearrange("(p j) f -> p j f", j=CHUNKS)
                                      ).then_inc(features_loaded[slot], 16)
                        act.dma_start(c.features[TAIL_PARTS:TAIL_PARTS + 1, slot, 0:TAIL_REST, :],
                                      edge_features[mid:EDGES, :].rearrange("(p j) f -> p j f", p=1)
                                      ).then_inc(features_loaded[slot], 16)

                    with act.Fori(0, rounds) as r:
                        act.wait_ge(rounds_done, r + 1)
                        act.sem_inc(gate, 1)
                        load(0, 0, r * GROUPS, False)
                        with act.Fori(0, TURNS - 1) as i:
                            for s in range(SLOTS):
                                load(i * SLOTS + (s + 1), (s + 1) % SLOTS, r * GROUPS + i * SLOTS + (s + 1), False)
                        for g in range(GROUPS - SLOTS, GROUPS):
                            load(g, g % SLOTS, r * GROUPS + g, g == GROUPS - 1)

            @block.gpsimd
            def _(pool):
                rounds = pool.value_load(c.rounds_i[0:1, 0:1], min_val=1, max_val=MAX_ROUNDS)

                def body(r, g, slot, t, use, first):
                    pool.wait_ge(idx_loaded[slot], use * 16 + 16)
                    pool.wait_ge(summed, t + 1)
                    pool.sem_inc(gate, 1)
                    for j in range(CHUNKS):
                        nc.gpsimd.indirect_dma_start(
                            c.rows[:, slot, j, :], None, c.table[:, :],
                            bass.IndirectOffsetOnAxis(ap=c.idx[:, slot, j:j + 1], axis=0)).then_inc(rows_gathered[slot], 16)
                each_group(pool, rounds, body)

            @block.tensor
            def _(pe):
                pe.sem_inc(summed, SLOTS)
                rounds = pe.value_load(c.rounds_i[0:1, 0:1], min_val=1, max_val=MAX_ROUNDS)

                def body(r, g, slot, t, use, first):
                    if edge_features is not None:
                        pe.wait_ge(messages_ready, t + 1 + SLOTS)
                    else:
                        pe.wait_ge(rows_gathered[slot], use * (16 * CHUNKS) + 16 * CHUNKS)
                    pe.wait_ge(onehot_ready, t + 1)
                    for j in range(CHUNKS):
                        last = nc.tensor.matmul(ps[slot][:, 0:WINDOW], c.rows[:, slot, j, :], hot[slot][:, j, :],
                                                start=(j == 0), stop=(j == CHUNKS - 1))
                    last.then_inc(summed, 1)
                each_group(pe, rounds, body)

            @block.vector
            def _(dve):
                dve.sem_inc(messages_ready, SLOTS)
                nc.vector.tensor_copy(c.iota[:, :], c.iota0[:, :]).then_inc(iota_reset, 1)
                if edge_features is not None:
                    nc.vector.tensor_scalar(acc, c.ht[:, :], 2.0, None, ALU.mult).then_inc(iota_reset, 1)
                else:
                    nc.vector.memset(acc, 0.0).then_inc(iota_reset, 1)
                dve.wait_ge(iota_reset, 2)
                dve.sem_inc(rounds_done, 1)
                rounds = dve.value_load(c.rounds_i[0:1, 0:1], min_val=1, max_val=MAX_ROUNDS)

                def add(g, slot, t):
                    base = dve.value_load(c.window[0:1, bass.ds(g, 1)], min_val=0, max_val=WINDOW_END)
                    dve.wait_ge(summed, t + 1 + SLOTS)
                    nc.vector.tensor_tensor(acc[:, bass.ds(base, WINDOW)], acc[:, bass.ds(base, WINDOW)],
                                            ps[slot][:, 0:WINDOW], ALU.add).then_inc(added, 1)
                    dve.wait_ge(added, t + 1)
                    dve.sem_inc(gate, 1)

                def body(r, g, slot, t, use, first):
                    if first:
                        dve.wait_ge(windows_loaded, r * 16 + 16)
                        dve.sem_inc(gate, 1)
                    made = nc.vector.scalar_tensor_tensor(
                        out=hot[slot],
                        in0=c.iota[:, :].unsqueeze(1).to_broadcast([P, CHUNKS, WINDOW]),
                        scalar=c.first[:, bass.ds(g, 1)],
                        in1=c.dst[:, bass.ds(g * CHUNKS, CHUNKS)].unsqueeze(2).to_broadcast([P, CHUNKS, WINDOW]),
                        op0=ALU.add, op1=ALU.is_equal)
                    if weighted_edges:
                        made.then_inc(match_ready, 1)
                        dve.wait_ge(match_ready, t + 1)
                        nc.vector.tensor_tensor(hot[slot], hot[slot],
                                                c.weight[:, bass.ds(g * CHUNKS, CHUNKS)].unsqueeze(2).to_broadcast([P, CHUNKS, WINDOW]),
                                                ALU.mult).then_inc(onehot_ready, 1)
                    else:
                        made.then_inc(onehot_ready, 1)
                    if edge_features is not None:
                        dve.wait_ge(rows_gathered[slot], use * (16 * CHUNKS) + 16 * CHUNKS)
                        dve.wait_ge(features_loaded[slot], use * 16 + (r * 16 if slot == (GROUPS - 1) % SLOTS else 0)
                                    + 16)
                        nc.vector.tensor_tensor(c.rows[:, slot, :, :], c.rows[:, slot, :, :], c.features[:, slot, :, :],
                                                ALU.add).then_inc(messages_ready, 1)
                    if not first:
                        add(g - 1, (slot + SLOTS - 1) % SLOTS, t - 1)

                with dve.Fori(0, rounds) as r:
                    body(r, 0, 0, r * GROUPS, r * USES[0], True)
                    with dve.Fori(0, TURNS - 1) as i:
                        for s in range(SLOTS):
                            slot = (s + 1) % SLOTS
                            body(r, i * SLOTS + (s + 1), slot, r * GROUPS + i * SLOTS + (s + 1),
                                 r * USES[slot] + i + (1 if slot == 0 else 0), False)
                    for g in range(GROUPS - SLOTS, GROUPS):
                        slot = g % SLOTS
                        if g == GROUPS - 1 and edge_features is not None:
                            dve.wait_ge(features_loaded[slot], (r + 1) * (16 * (USES[slot] + 1)))
                        body(r, g, slot, r * GROUPS + g, r * USES[slot] + g // SLOTS, False)
                    add(GROUPS - 1, (GROUPS - 1) % SLOTS, r * GROUPS + (GROUPS - 1))
                    nc.vector.tensor_scalar(c.iota[:, :], c.iota[:, :], float(WINDOW), None, ALU.add).then_inc(iota_moved, 1)
                    dve.wait_ge(iota_moved, r + 1)
                    dve.sem_inc(rounds_done, 1)


def scatter_stage(nc, c):
    with semaphores(nc, "s_") as sem:
        rounds_done, windows_loaded, gate = sem("rounds_done"), sem("windows_loaded"), c.gate
        h_loaded = [sem(f"h_loaded{s}") for s in range(SLOTS)]
        PER_GROUP = 16 * (CHUNKS // REPLICAS)
        landed = [sem(f"landed{j}") for j in range(REPLICAS)]
        onehot_ready, source_ready, source_turned = sem("onehot_ready"), sem("source_ready"), sem("source_turned")
        same_ready, counts_ready, counts_copied, messages_made = sem("same_ready"), sem("counts_ready"), sem("counts_copied"), sem("messages_made")
        messages_ready, earlier_ready, earlier_counted = sem("messages_ready"), sem("earlier_ready"), sem("earlier_counted")
        detour_ready, detour_taken, rows_named = sem("detour_ready"), sem("detour_taken"), sem("rows_named")
        round_landed = sem("round_landed")
        messages_landed, iota_reset, iota_moved = sem("messages_landed"), sem("iota_reset"), sem("iota_moved")
        psR, psC, psG = c.psum_wide[0], c.psum_wide[1], c.psum_wide[2]
        hot = c.onehot[:, 0:256].bitcast(BF16)
        hot3 = hot.rearrange("p (j w) -> p j w", w=WINDOW)
        same = c.onehot[:, 256:768].bitcast(BF16)
        same3 = same.rearrange("p (j k) -> p j k", k=P)
        earlier = c.onehot[:, 768:1280].bitcast(BF16)
        earlier3 = earlier.rearrange("p (j k) -> p j k", k=P)
        hwin = c.features[:, 1, :, :]
        now, cnt, det = c.small[:, 0:8], c.small[:, 8:16], c.small[:, 16:24]
        with nc.Block() as block:
            @block.sync
            def _(sp):
                rounds = sp.value_load(c.rounds_i[0:1, 0:1], min_val=1, max_val=MAX_ROUNDS)

                def body(r, g, slot, t, use, first):
                    if first:
                        windows_program(sp, c, rounds_done, windows_loaded, r)
                        sp.wait_ge(windows_loaded, r * 16 + 16)
                        sp.sem_inc(gate, 1)
                    base = sp.value_load(c.window[0:1, bass.ds(g, 1)], min_val=0, max_val=WINDOW_END)
                    sp.wait_ge(messages_made, t + 1)
                    sp.dma_start(hwin[0:WINDOW, slot, :], c.table[bass.ds(base, WINDOW), :]).then_inc(h_loaded[slot], 16)
                each_group(sp, rounds, body)

            @block.gpsimd
            def _(pool):
                for j in range(REPLICAS):
                    pool.dma_start(c.replicas[j][NODES:NODES + P, :], c.zeros).then_inc(landed[j], 16)
                pool.sem_inc(messages_landed, 2)
                rounds = pool.value_load(c.rounds_i[0:1, 0:1], min_val=1, max_val=MAX_ROUNDS)

                def body(r, g, slot, t, use, first):
                    pool.wait_ge(messages_ready, t + 1)
                    pool.wait_ge(rows_named, t + 1 + SLOTS)
                    pool.sem_inc(gate, 1)
                    for j in range(CHUNKS):
                        k = j % REPLICAS
                        pool.wait_ge(landed[k], t * PER_GROUP + (j // REPLICAS + 1) * 16)
                        pool.sem_inc(gate, 1)
                        nc.gpsimd.indirect_dma_start(
                            c.replicas[k][:, :], bass.IndirectOffsetOnAxis(ap=c.idx[:, slot, j:j + 1], axis=0),
                            c.rows[:, slot, j, :], None, compute_op=ALU.add).then_inc(landed[k], 16)
                    pool.sem_inc(messages_landed, 1)
                with pool.Fori(0, rounds) as r:
                    body(r, 0, 0, r * GROUPS, None, True)
                    with pool.Fori(0, TURNS) as i:
                        for s in range(SLOTS):
                            body(r, None, (s + 1) % SLOTS, r * GROUPS + i * SLOTS + (s + 1), None, False)
                    for j in range(REPLICAS):
                        pool.wait_ge(landed[j], r * (PER_GROUP * GROUPS) + (PER_GROUP * GROUPS + 16))
                    pool.sem_inc(round_landed, 1)

            @block.tensor
            def _(pe):
                pe.sem_inc(messages_made, SLOTS)
                pe.sem_inc(counts_ready, 1)
                rounds = pe.value_load(c.rounds_i[0:1, 0:1], min_val=1, max_val=MAX_ROUNDS)

                def make_messages(slot, t, r, use):
                    pe.wait_ge(counts_copied, t + 2)
                    pe.wait_ge(h_loaded[slot], use * 16 + 16)
                    for j in range(CHUNKS):
                        last = nc.tensor.matmul(psG[:, j * P:(j + 1) * P], c.turned[0:WINDOW, j * P:(j + 1) * P],
                                                hwin[0:WINDOW, slot, :], start=True, stop=True)
                    last.then_inc(messages_made, 1)

                def body(r, slot, t, first, use_before):
                    pe.wait_ge(source_ready, t + 1)
                    for j in range(CHUNKS):
                        last = nc.tensor.transpose(psR[:, j * P:(j + 1) * P], now[:, j:j + 1].to_broadcast([P, P]),
                                                   c.ident[:, :])
                    last.then_inc(source_turned, 1)
                    if not first:
                        make_messages((slot + SLOTS - 1) % SLOTS, t - 1, r, use_before)
                    pe.wait_ge(same_ready, t + 1)
                    pe.wait_ge(counts_copied, t + 1)
                    for j in range(CHUNKS):
                        last = nc.tensor.matmul(psC[0:WINDOW, j * P:(j + 1) * P], hot3[:, j, :], same3[:, j, :],
                                                start=True, stop=True)
                    last.then_inc(counts_ready, 1)

                with pe.Fori(0, rounds) as r:
                    body(r, 0, r * GROUPS, True, None)
                    with pe.Fori(0, TURNS) as i:
                        for s in range(SLOTS):
                            body(r, (s + 1) % SLOTS, r * GROUPS + i * SLOTS + (s + 1), False, r * USES[s] + i)
                    last_slot = (GROUPS - 1) % SLOTS
                    make_messages(last_slot, r * GROUPS + (GROUPS - 1), r, r * USES[last_slot] + (GROUPS - 1) // SLOTS)

            @block.scalar
            def _(act):
                act.sem_inc(counts_copied, 1)
                rounds = act.value_load(c.rounds_i[0:1, 0:1], min_val=1, max_val=MAX_ROUNDS)

                def copy_messages(slot, t):
                    act.wait_ge(messages_made, t + 1 + SLOTS)
                    act.wait_ge(messages_landed, t + 1)
                    nc.scalar.activation(c.rows[:, slot, :, :].rearrange("p j f -> p (j f)"), psG[:, :],
                                         ACT.Copy).then_inc(messages_ready, 1)

                def copy_counts(t):
                    act.wait_ge(counts_ready, t + 2)
                    act.wait_ge(messages_made, t + SLOTS)
                    nc.scalar.activation(c.turned[0:WINDOW, :], psC[0:WINDOW, :], ACT.Copy).then_inc(counts_copied, 1)

                with act.Fori(0, rounds) as r:
                    copy_counts(r * GROUPS)
                    with act.Fori(0, TURNS) as i:
                        for s in range(SLOTS):
                            copy_messages(s, r * GROUPS + i * SLOTS + s)
                            copy_counts(r * GROUPS + i * SLOTS + (s + 1))
                    copy_messages((GROUPS - 1) % SLOTS, r * GROUPS + (GROUPS - 1))

            @block.vector
            def _(dve):
                dve.sem_inc(rows_named, SLOTS)
                nc.vector.tensor_copy(c.iota[:, :], c.iota0[:, :]).then_inc(iota_reset, 1)
                dve.wait_ge(iota_reset, 1)
                dve.sem_inc(rounds_done, 1)
                rounds = dve.value_load(c.rounds_i[0:1, 0:1], min_val=1, max_val=MAX_ROUNDS)

                def body(r, g, slot, t, use, first):
                    nc.vector.tensor_copy(now, c.src_i[:, bass.ds(g * CHUNKS, CHUNKS)]).then_inc(source_ready, 1)
                    dve.wait_ge(counts_ready, t + 1)
                    nc.vector.scalar_tensor_tensor(
                        out=hot3,
                        in0=c.iota[:, :].unsqueeze(1).to_broadcast([P, CHUNKS, WINDOW]),
                        scalar=c.first[:, bass.ds(g, 1)],
                        in1=c.dst[:, bass.ds(g * CHUNKS, CHUNKS)].unsqueeze(2).to_broadcast([P, CHUNKS, WINDOW]),
                        op0=ALU.add, op1=ALU.is_equal).then_inc(onehot_ready, 1)
                    dve.wait_ge(source_ready, t + 1)
                    dve.wait_ge(source_turned, t + 1)
                    nc.vector.tensor_tensor(same3, psR[:, :].rearrange("p (j k) -> p j k", k=P),
                                            now.unsqueeze(2).to_broadcast([P, CHUNKS, P]),
                                            ALU.is_equal).then_inc(same_ready, 1)
                    dve.wait_ge(same_ready, t + 1)
                    nc.vector.tensor_tensor(earlier3, same3, c.before[:, :].unsqueeze(1).to_broadcast([P, CHUNKS, P]),
                                            ALU.mult).then_inc(earlier_ready, 1)
                    nc.vector.tensor_scalar(det, now, -1.0, c.dump[:, :], ALU.mult, ALU.add).then_inc(detour_ready, 1)
                    dve.wait_ge(earlier_ready, t + 1)
                    nc.vector.tensor_reduce(cnt, earlier3, AX.X, ALU.add).then_inc(earlier_counted, 1)
                    dve.wait_ge(detour_ready, t + 1)
                    dve.wait_ge(earlier_counted, t + 1)
                    nc.vector.scalar_tensor_tensor(out=det, in0=cnt, scalar=1.0, in1=det, op0=ALU.min,
                                                   op1=ALU.mult).then_inc(detour_taken, 1)
                    dve.wait_ge(detour_taken, t + 1)
                    dve.wait_ge(messages_landed, t + 1)
                    nc.vector.tensor_tensor(c.idx[:, slot, :], det, now, ALU.add).then_inc(rows_named, 1)
                    dve.wait_ge(rows_named, t + 1 + SLOTS)
                    dve.sem_inc(gate, 1)

                with dve.Fori(0, rounds) as r:
                    body(r, 0, 0, r * GROUPS, r * USES[0], True)
                    with dve.Fori(0, TURNS) as i:
                        for s in range(SLOTS):
                            slot = (s + 1) % SLOTS
                            body(r, i * SLOTS + (s + 1), slot, r * GROUPS + i * SLOTS + (s + 1),
                                 r * USES[slot] + i + (1 if slot == 0 else 0), False)
                    nc.vector.tensor_scalar(c.iota[:, :], c.iota[:, :], float(WINDOW), None, ALU.add).then_inc(iota_moved, 1)
                    dve.wait_ge(iota_moved, r + 1)
                    dve.wait_ge(messages_made, r * GROUPS + (GROUPS + SLOTS))
                    dve.wait_ge(round_landed, r + 1)
                    dve.sem_inc(rounds_done, 1)


def divide_stage(nc, c):
    num, den = c.pair[:, 0:NODES_PAD], c.pair[:, NODES_PAD:]
    with semaphores(nc, "divide_") as sem:
        guarded, inverted, divided, x_back = sem("guarded"), sem("inverted"), sem("divided"), sem("x_back")
        with nc.Block() as block:
            @block.vector
            def _(dve):
                nc.vector.tensor_scalar(den, den, 1e-30, None, ALU.max).then_inc(guarded, 1)
                dve.wait_ge(guarded, 1)
                nc.vector.reciprocal(den, den).then_inc(inverted, 1)
                dve.wait_ge(inverted, 1)
                nc.vector.tensor_tensor(num, num, den, ALU.mult).then_inc(divided, 1)

            @block.sync
            def _(sp):
                sp.dma_start(c.x[:, :], c.x_store[:, :]).then_inc(x_back, 16)
                sp.wait_ge(x_back, 16)


def leaky_stage(nc, c, buf):
    with semaphores(nc) as sem:
        leaked = sem("leaked")
        with nc.Block() as block:
            @block.vector
            def _(dve):
                nc.vector.scalar_tensor_tensor(out=buf, in0=buf, scalar=0.01, in1=buf, op0=ALU.mult,
                                               op1=ALU.max).then_inc(leaked, 1)
                dve.wait_ge(leaked, 1)


def gather_replicas_stage(nc, c):
    halves = [c.pair[:, 0:NODES_PAD], c.pair[:, NODES_PAD:]]
    with semaphores(nc, "replicas_") as sem:
        loaded = [sem(f"loaded{k}") for k in range(2)]
        summed, first_loaded = sem("summed"), sem("first_loaded")
        rows = [rep[:, :].rearrange("(t p) f -> p t f", p=P) for rep in c.replicas]
        with nc.Block() as block:
            @block.sync
            def _(sp):
                sp.dma_start(tile_view(c.rows2), rows[0]).then_inc(first_loaded, 16)
                for k in range(1, REPLICAS):
                    if k >= 3:
                        sp.wait_ge(summed, k - 2)
                    sp.dma_start(halves[k % 2].rearrange("p (t f) -> p t f", f=D), rows[k]).then_inc(loaded[k % 2], 16)

            @block.vector
            def _(dve):
                dve.wait_ge(first_loaded, 16)
                for k in range(1, REPLICAS):
                    dve.wait_ge(loaded[k % 2], 16 * ((k + 1) // 2))
                    nc.vector.tensor_tensor(c.rows2[:, :], c.rows2[:, :], halves[k % 2], ALU.add).then_inc(summed, 1)
                    dve.wait_ge(summed, k)


def one_plus_eps_stage(nc, c):
    with semaphores(nc, "eps_") as sem:
        spread, made = sem("spread"), sem("made")
        with nc.Block() as block:
            @block.tensor
            def _(pe):
                nc.tensor.matmul(c.psum[0][:, 0:1], c.ones[0:1, :], c.eps_one[:, :], start=True, stop=True).then_inc(spread, 1)

            @block.vector
            def _(dve):
                nc.vector.memset(c.eps_col[:, :], LN_EPS).then_inc(made, 1)
                dve.wait_ge(spread, 1)
                nc.vector.tensor_scalar(c.eps_plus[:, :], c.psum[0][:, 0:1], 1.0, None, ALU.add).then_inc(made, 1)
                dve.wait_ge(made, 2)


def batchnorm_stage(nc, c, name, buf, gamma, beta):
    pieces = 25
    width = NODES // pieces
    stats = c.turned[:, 0:6 * pieces]
    mv, root, scale, shift = c.turned[:, 160:162], c.turned[:, 162:163], c.turned[:, 163:164], c.turned[:, 164:165]
    inv = c.turned[:, 165:166]
    with semaphores(nc, name + "_") as sem:
        piece_done, aggregated, rooted, scaled, applied, step = (sem("piece_done"), sem("aggregated"), sem("rooted"),
                                                                sem("scaled"), sem("applied"), sem("step"))
        with nc.Block() as block:
            @block.vector
            def _(dve):
                for k in range(pieces):
                    nc.vector.bn_stats(stats[:, 6 * k:6 * k + 6], buf[:, k * width:(k + 1) * width]).then_inc(piece_done, 1)
                dve.wait_ge(piece_done, pieces)
                nc.vector.bn_aggr(mv, stats).then_inc(aggregated, 1)
                dve.wait_ge(rooted, 1)
                nc.vector.reciprocal(inv, root).then_inc(step, 1)
                dve.wait_ge(step, 1)
                nc.vector.tensor_tensor(scale, inv, gamma, ALU.mult).then_inc(step, 1)
                dve.wait_ge(step, 2)
                nc.vector.tensor_tensor(shift, mv[:, 0:1], scale, ALU.mult).then_inc(step, 1)
                dve.wait_ge(step, 3)
                nc.vector.tensor_tensor(shift, beta, shift, ALU.subtract).then_inc(scaled, 1)

            @block.scalar
            def _(act):
                act.wait_ge(aggregated, 1)
                nc.scalar.activation(root, mv[:, 1:2], ACT.Sqrt, bias=c.eps_col[:, :]).then_inc(rooted, 1)
                act.wait_ge(scaled, 1)
                nc.scalar.activation(buf, buf, ACT.Relu, scale=scale, bias=shift).then_inc(applied, 1)
                act.wait_ge(applied, 1)


def store_stage(nc, c, out):
    with semaphores(nc) as sem:
        stored = sem("out_stored")
        with nc.Block() as block:
            @block.sync
            def _(sp):
                full, rest = node_rows(out)
                sp.dma_start(full, tile_view(c.x)[:, 0:FULL_TILES, :]).then_inc(stored, 16)
                sp.dma_start(rest, tile_view(c.x)[0:TAIL, FULL_TILES, :]).then_inc(stored, 16)
                sp.wait_ge(stored, 32)


def gnn_program(nc, io, out):
    c = Core()
    with ExitStack() as ctx:
        sb = lambda n, shape, dt=F32: ctx.enter_context(nc.sbuf_tensor(n, shape, dt))
        c.gate = ctx.enter_context(nc.semaphore("gate"))
        c.x = sb("x_rows", [P, NODES_PAD])
        c.ht = sb("h_columns", [P, NODES_PAD])
        c.pair = sb("pair", [P, 2 * NODES_PAD])
        c.maxima = sb("maxima", [P, NODES_PAD])
        c.rows1 = c.pair[:, NODES_PAD:]
        c.rows2 = c.maxima
        c.temp = c.ht
        c.src_i = sb("src_i", [P, GROUPS * CHUNKS], I32)
        c.dst = sb("dst", [P, GROUPS * CHUNKS])
        c.weight = sb("edge_w", [P, GROUPS * CHUNKS])
        c.first = sb("first_dst", [P, GROUPS])
        c.window = sb("window", [1, GROUPS], I32)
        c.rounds_i = sb("rounds_i", [P, 1], I32)
        c.rows = sb("gathered_rows", [P, SLOTS, CHUNKS, D])
        c.features = sb("edge_features", [P, SLOTS, CHUNKS, D])
        c.turned = c.features[:, 0, :, :].rearrange("p j f -> p (j f)")
        c.onehot = sb("onehot", [P, (SLOTS * CHUNKS + 1) * WINDOW])
        c.idx = sb("idx", [P, SLOTS, CHUNKS], I32)
        c.small = sb("small", [P, 640])
        c.ident = sb("ident", [P, P])
        c.ones = sb("ones", [P, P])
        c.zeros2 = sb("zeros", [P, 2 * D])
        c.zeros = c.zeros2[:, 0:D]
        c.before = sb("before", [P, P])
        c.iota0 = sb("iota0", [P, WINDOW])
        c.iota = sb("iota", [P, WINDOW])
        c.dump = sb("dump", [P, 1])
        c.stat_a = sb("stat_a", [P, TILES])
        c.stat_b = sb("stat_b", [P, TILES])
        c.eps_col = sb("eps_col", [P, 1])
        c.eps_plus = sb("eps_plus", [P, 1])
        c.eps_one = sb("eps_one", [1, 1])
        c.weight_names = ["L0_gnn_Wq", "L0_gnn_Wk", "L0_gnn_Wv", "L0_gnn_Wo", "L1_gnn_W1", "L1_gnn_W2",
                          "L2_gnn_w1", "L2_gnn_w2"]
        c.column_names = ["L1_gnn_b1", "L1_gnn_b2", "L2_gnn_b1", "L2_gnn_gamma1", "L2_gnn_beta1",
                          "L2_gnn_b2", "L2_gnn_gamma2", "L2_gnn_beta2"]
        c.mats = sb("mats", [P, len(c.weight_names), D])
        c.cols = sb("cols", [P, len(c.column_names)])
        c.setup_loads = 3 + 1 + len(c.weight_names) + len(c.column_names) + 1 + 1
        ps = ctx.enter_context(nc.psum_tensor("ps", [P, 8, 512], F32))
        c.psum = [ps[:, k, :] for k in range(8)]
        flat = ps[:, :, :].rearrange("p b n -> p (b n)")
        c.psum_wide = [flat[:, 1024 * k:1024 * (k + 1)] for k in range(4)]
        c.table = nc.dram_tensor("h_table", (NODES_PAD, D), F32).ap()
        c.x_store = nc.dram_tensor("x_store", (P, NODES_PAD), F32).ap()
        c.window_table = nc.dram_tensor("window_table", (MAX_ROUNDS, GROUPS), I32).ap()
        c.replicas = [nc.dram_tensor(f"replica{j}", (NODES_PAD, D), F32).ap() for j in range(REPLICAS)]
        mat = lambda n: c.mats[:, c.weight_names.index(n), :]
        col = lambda n: c.cols[:, c.column_names.index(n):c.column_names.index(n) + 1]
        ht, num, acc2 = c.ht, c.pair[:, 0:NODES_PAD], c.pair[:, NODES_PAD:]
        add_to_x = lambda cols, p: nc.vector.tensor_tensor(c.x[:, cols], c.x[:, cols], p, ALU.add)
        to_ht = lambda cols, p: nc.vector.tensor_copy(ht[:, cols], p)

        setup_stage(nc, c, io)
        one_plus_eps_stage(nc, c)

        normalise_stage(nc, c, "n0", keep_x=True)
        turn_stage(nc, c, "t0", c.rows2, to_ht)
        wkt = c.small[:, 0:P]
        with semaphores(nc) as sem:
            wk_turned, wk_copied = sem("wk_turned"), sem("wk_copied")
            with nc.Block() as block:
                @block.tensor
                def _(pe):
                    nc.tensor.transpose(c.psum[0][:, 0:P], mat("L0_gnn_Wk"), c.ident[:, :]).then_inc(wk_turned, 1)

                @block.vector
                def _(dve):
                    dve.wait_ge(wk_turned, 1)
                    nc.vector.tensor_copy(wkt, c.psum[0][:, 0:P]).then_inc(wk_copied, 1)
                    dve.wait_ge(wk_copied, 1)
        project_stage(nc, c, "q", mat("L0_gnn_Wq"), ht, lambda s, p: nc.scalar.activation(num[:, s], p, ACT.Copy))
        project_stage(nc, c, "g", wkt, num,
                      lambda s, p: nc.scalar.activation(c.x[:, s], p, ACT.Copy, scale=float(D) ** -0.5))
        attention_stage(nc, c)
        divide_stage(nc, c)
        project_stage(nc, c, "v", mat("L0_gnn_Wv"), num, lambda s, p: nc.scalar.activation(acc2[:, s], p, ACT.Copy))
        project_stage(nc, c, "o", mat("L0_gnn_Wo"), acc2, lambda s, p: nc.scalar.activation(num[:, s], p, ACT.Copy))
        with semaphores(nc) as sem:
            h_added = sem("h_added")
            with nc.Block() as block:
                @block.vector
                def _(dve):
                    nc.vector.tensor_tensor(num, num, ht[:, :], ALU.add).then_inc(h_added, 1)
                    dve.wait_ge(h_added, 1)
        turn_stage(nc, c, "b0", num, add_to_x)

        normalise_stage(nc, c, "n1")
        turn_stage(nc, c, "t1", c.rows2, to_ht)
        sum_stage(nc, c, "m1", num, edge_features=io["edge_attr_128"])
        project_stage(nc, c, "p1", mat("L1_gnn_W1"), num,
                      lambda s, p: nc.scalar.activation(acc2[:, s], p, ACT.Identity, bias=col("L1_gnn_b1")))
        leaky_stage(nc, c, acc2)
        project_stage(nc, c, "p2", mat("L1_gnn_W2"), acc2,
                      lambda s, p: nc.scalar.activation(num[:, s], p, ACT.Identity, bias=col("L1_gnn_b2")))
        turn_stage(nc, c, "b1", num, add_to_x)

        normalise_stage(nc, c, "n2")
        turn_stage(nc, c, "t2", c.rows2, to_ht)
        scatter_stage(nc, c)
        gather_replicas_stage(nc, c)
        turn_stage(nc, c, "a2", c.rows2,
                   lambda cols, p: nc.vector.scalar_tensor_tensor(out=num[:, cols], in0=ht[:, cols],
                                                                  scalar=c.eps_plus[:, :], in1=p,
                                                                  op0=ALU.mult, op1=ALU.add))
        project_stage(nc, c, "p3", mat("L2_gnn_w1"), num,
                      lambda s, p: nc.scalar.activation(acc2[:, s], p, ACT.Identity, bias=col("L2_gnn_b1")))
        batchnorm_stage(nc, c, "bn1", acc2, col("L2_gnn_gamma1"), col("L2_gnn_beta1"))
        project_stage(nc, c, "p4", mat("L2_gnn_w2"), acc2,
                      lambda s, p: nc.scalar.activation(num[:, s], p, ACT.Identity, bias=col("L2_gnn_b2")))
        batchnorm_stage(nc, c, "bn2", num, col("L2_gnn_gamma2"), col("L2_gnn_beta2"))
        turn_stage(nc, c, "b2", num, add_to_x)

        normalise_stage(nc, c, "n3")
        sum_stage(nc, c, "m3", num, weighted_edges=True)
        turn_stage(nc, c, "b3", num, add_to_x)
        store_stage(nc, c, out)


_INS = ["x", "src", "dst", "edge_attr_128", "edge_weight", "L0_gnn_Wq", "L0_gnn_Wk", "L0_gnn_Wv", "L0_gnn_Wo",
        "L1_gnn_W1", "L1_gnn_b1", "L1_gnn_W2", "L1_gnn_b2", "L2_gnn_eps", "L2_gnn_w1", "L2_gnn_b1",
        "L2_gnn_gamma1", "L2_gnn_beta1", "L2_gnn_w2", "L2_gnn_b2", "L2_gnn_gamma2", "L2_gnn_beta2"]


def kernel(**inputs):
    import numpy as _np
    import concourse.bacc as _bacc
    from concourse import mybir as _mybir
    from concourse.bass_utils import run_bass_kernel_spmd as _run

    nc = _bacc.Bacc("TRN2", target_bir_lowering=False, num_devices=1)
    arrays, io = {}, {}
    for name in _INS:
        a = _np.ascontiguousarray(inputs[name])
        arrays[f"in_{name}_dram"] = a
        io[name] = nc.dram_tensor(f"in_{name}_dram", a.shape, _mybir.dt.from_np(a.dtype), kind="ExternalInput").ap()
    out = nc.dram_tensor("out_dram", (NODES, D), _mybir.dt.float32, kind="ExternalOutput").ap()
    gnn_program(nc, io, out)
    r = _run(nc, [arrays], core_ids=[0])
    return r.results[0]["out_dram"]
```

```python
import concourse.bass as bass
from concourse import mybir
from contextlib import ExitStack, contextmanager

F32 = mybir.dt.float32
BF16 = mybir.dt.bfloat16
I32 = mybir.dt.int32
ALU = mybir.AluOpType
ACT = mybir.ActivationFunctionType
AX = mybir.AxisListType

P = 128
D = 128
NODES = 6250
EDGES = 206250
TILES = 50
FULL_TILES = NODES // P
TAIL = NODES - FULL_TILES * P
NODES_PAD = TILES * P
CHUNKS = 8
GROUP = P * CHUNKS
GROUPS = -(-EDGES // GROUP)
FULL_GROUPS = EDGES // GROUP
TAIL_EDGES = EDGES - FULL_GROUPS * GROUP
TAIL_PARTS = TAIL_EDGES // CHUNKS
TAIL_REST = TAIL_EDGES - TAIL_PARTS * CHUNKS
WINDOW = 64
WINDOW_END = 6256
MAX_ROUNDS = NODES // WINDOW + 1
SLOTS = 4
TURNS = (GROUPS - 2) // SLOTS
assert 1 + TURNS * SLOTS + 1 == GROUPS
USES = [len(range(s, GROUPS, SLOTS)) for s in range(SLOTS)]
REPLICAS = CHUNKS // 2
FAR = -1e30
FLOOR = -1e29
LN_EPS = 1e-5
BN_EPS = 1e-5


def each_group(eng, rounds, body, finish=None):
    with eng.Fori(0, rounds) as r:
        body(r, 0, 0, r * GROUPS, r * USES[0], True)
        with eng.Fori(0, TURNS) as i:
            for s in range(SLOTS):
                slot = (s + 1) % SLOTS
                body(r, i * SLOTS + (s + 1), slot, r * GROUPS + i * SLOTS + (s + 1),
                     r * USES[slot] + i + (1 if slot == 0 else 0), False)
        g = GROUPS - 1
        body(r, g, g % SLOTS, r * GROUPS + g, r * USES[g % SLOTS] + g // SLOTS, False)
        if finish:
            finish(r)


def is_last(g):
    return isinstance(g, int) and g == GROUPS - 1


class Core:
    pass


@contextmanager
def semaphores(nc, prefix=""):
    taken = []

    def sem(name):
        taken.append(nc.alloc_semaphore(prefix + name))
        return taken[-1]

    yield sem
    nc.clear_and_free_semaphores(taken)
    nc.all_engine_barrier()


def node_rows(table):
    return (table[0:FULL_TILES * P, :].rearrange("(t p) f -> p t f", p=P),
            table[FULL_TILES * P:NODES, :])


def tile_view(buf):
    return buf[:, :].rearrange("p (t f) -> p t f", f=D)


def setup_stage(nc, c, io):
    with semaphores(nc) as sem:
        loaded, tails, stored = sem("loaded"), sem("tails"), sem("stored")
        pads_set, zeros_set, iotas_made = sem("pads_set"), sem("zeros_set"), sem("iotas_made")
        masks_cleared, masks_made = sem("masks_cleared"), sem("masks_made")
        dve_step, turned = sem("setup_dve_step"), sem("setup_turned")
        dst_i = c.temp[:, 0:GROUPS * CHUNKS].bitcast(I32)
        edge_lo = c.temp[:, 2048:2048 + 2 * P]
        edge_hi = c.temp[:, 2304:2304 + 2 * P]
        ends = c.temp[:, 2560:2564]
        top_f = c.temp[:, 2600:2600 + GROUPS]
        table_i = c.temp[:, 3000:3000 + GROUPS].bitcast(I32)
        widest = c.temp[:, 3300:3301]
        widest_i = c.temp[:, 3301:3302].bitcast(I32)
        iota_i = c.temp[:, 3400:3400 + WINDOW].bitcast(I32)
        part_i = c.temp[:, 3500:3501].bitcast(I32)
        shift_f = c.temp[:, 3501:3502]
        ps = c.psum[0]

        with nc.Block() as block:
            @block.sync
            def _(sp):
                pair = lambda a: a[0:FULL_GROUPS * GROUP].rearrange("(g p j) -> p g j", p=P, j=CHUNKS)
                whole = FULL_GROUPS * CHUNKS
                for name, src, dst in (("src", io["src"], c.src_i), ("dst", io["dst"], dst_i),
                                       ("w", io["edge_weight"], c.weight)):
                    sp.dma_start(dst[:, 0:whole].rearrange("p (g j) -> p g j", j=CHUNKS),
                                 pair(src)).then_inc(loaded, 16)
                sp.wait_ge(pads_set, 3)
                for src, dst in ((io["src"], c.src_i), (io["dst"], dst_i), (io["edge_weight"], c.weight)):
                    at = FULL_GROUPS * GROUP
                    mid = at + TAIL_PARTS * CHUNKS
                    sp.dma_start(dst[0:TAIL_PARTS, whole:whole + CHUNKS],
                                 src[at:mid].rearrange("(p j) -> p j", j=CHUNKS)).then_inc(tails, 16)
                    sp.dma_start(dst[TAIL_PARTS:TAIL_PARTS + 1, whole:whole + TAIL_REST],
                                 src[mid:EDGES].rearrange("(p j) -> p j", p=1)).then_inc(tails, 16)
                sp.wait_ge(dve_step, 8)
                sp.dma_start(c.window_table[:, :], table_i[0:MAX_ROUNDS, :]).then_inc(stored, 16)
                sp.wait_ge(stored, 16 * 2)

            @block.scalar
            def _(act):
                full, rest = node_rows(io["x"])
                act.dma_start(tile_view(c.x)[:, 0:FULL_TILES, :], full).then_inc(loaded, 16)
                for k, name in enumerate(c.weight_names):
                    act.dma_start(c.mats[:, k, :], io[name]).then_inc(loaded, 16)
                for k, name in enumerate(c.column_names):
                    act.dma_start(c.cols[:, k:k + 1],
                                  io[name].rearrange("(p o) -> p o", o=1)).then_inc(loaded, 16)
                act.dma_start(c.eps_one[:, :], io["L2_gnn_eps"].rearrange("(a b) -> a b", a=1)).then_inc(loaded, 16)
                act.wait_ge(zeros_set, 1)
                act.dma_start(c.x[0:TAIL, FULL_TILES * D:(FULL_TILES + 1) * D], rest).then_inc(loaded, 16)
                act.wait_ge(zeros_set, 2)
                act.dma_start(c.table[NODES:NODES_PAD, :].rearrange("(p a) f -> p (a f)", a=2),
                              c.zeros2[0:(NODES_PAD - NODES) // 2, :]).then_inc(stored, 16)

            @block.gpsimd
            def _(pool):
                for m in (c.ident, c.before):
                    nc.gpsimd.memset(m[:, :], 0.0).then_inc(masks_cleared, 1)
                nc.gpsimd.memset(c.ones[:, :], 1.0).then_inc(masks_cleared, 1)
                pool.wait_ge(masks_cleared, 3)
                nc.gpsimd.affine_select(out=c.ident[:, :], in_=c.ident[:, :], compare_op=ALU.not_equal, fill=1.0,
                                        base=0, pattern=[[-1, P]], channel_multiplier=1).then_inc(masks_made, 1)
                nc.gpsimd.affine_select(out=c.before[:, :], in_=c.before[:, :], compare_op=ALU.is_ge, fill=1.0,
                                        base=0, pattern=[[1, P]], channel_multiplier=-1).then_inc(masks_made, 1)
                nc.gpsimd.iota(iota_i, [[1, WINDOW]], base=0, channel_multiplier=0).then_inc(iotas_made, 1)
                nc.gpsimd.iota(part_i, [[1, 1]], base=0, channel_multiplier=1).then_inc(iotas_made, 1)

            @block.vector
            def _(dve):
                done = [0]

                def link(ins):
                    done[0] += 1
                    ins.then_inc(dve_step, 1)
                    dve.wait_ge(dve_step, done[0])

                nc.vector.memset(c.x[:, FULL_TILES * D:], 0.0).then_inc(zeros_set, 1)
                nc.vector.memset(c.zeros2[:, :], 0.0).then_inc(zeros_set, 1)
                whole = FULL_GROUPS * CHUNKS
                nc.vector.memset(c.src_i[:, whole:], 0).then_inc(pads_set, 1)
                nc.vector.memset(dst_i[:, whole:], NODES).then_inc(pads_set, 1)
                nc.vector.memset(c.weight[:, whole:], 0.0).then_inc(pads_set, 1)
                nc.vector.memset(edge_lo[:, :], 0.0)
                link(nc.vector.memset(edge_hi[:, :], 0.0))
                dve.wait_ge(loaded, 16 * c.setup_loads)
                dve.wait_ge(tails, 16 * 6)
                link(nc.vector.tensor_copy(c.dst[:, :], dst_i))
                by_group = c.dst[:, :].rearrange("p (g j) -> p g j", j=CHUNKS)
                nc.vector.tensor_reduce(edge_lo[:, 0:GROUPS], by_group, AX.X, ALU.min)
                link(nc.vector.tensor_reduce(edge_hi[:, 0:GROUPS], by_group, AX.X, ALU.max))
                dve.wait_ge(turned, 1)
                for k, op in enumerate((ALU.min, ALU.min, ALU.max, ALU.max)):
                    last = nc.vector.tensor_reduce(ends[:, k:k + 1], ps[:, k * P:(k + 1) * P], AX.X, op)
                link(last)
                dve.wait_ge(turned, 2)
                nc.vector.tensor_copy(c.first[:, :], ps[:, 0:GROUPS])
                link(nc.vector.tensor_copy(top_f, ps[:, 2 * P:2 * P + GROUPS]))
                dve.wait_ge(iotas_made, 2)
                nc.vector.tensor_copy(c.iota0[:, :], iota_i)
                nc.vector.tensor_scalar(c.dump[:, :], part_i, float(NODES), None, ALU.add)
                nc.vector.tensor_scalar(shift_f, part_i, float(WINDOW), None, ALU.mult)
                link(nc.vector.tensor_tensor(top_f, top_f, c.first[:, :], ALU.subtract))
                link(nc.vector.tensor_reduce(widest, top_f, AX.X, ALU.max))
                link(nc.vector.tensor_scalar(table_i, c.first[:, :], shift_f, float(WINDOW_END), ALU.add, ALU.min))
                link(nc.vector.tensor_copy(widest_i, widest))
                link(nc.vector.tensor_scalar(c.rounds_i[:, :], widest_i, 6, None, ALU.arith_shift_right))
                link(nc.vector.tensor_scalar(c.rounds_i[:, :], c.rounds_i[:, :], 1.0, None, ALU.add))

            @block.tensor
            def _(pe):
                pe.wait_ge(masks_made, 2)
                pe.wait_ge(dve_step, 3)
                for k, part in enumerate((edge_lo[:, 0:P], edge_lo[:, P:2 * P], edge_hi[:, 0:P], edge_hi[:, P:2 * P])):
                    last = nc.tensor.transpose(ps[:, k * P:(k + 1) * P], part, c.ident[:, :])
                last.then_inc(turned, 1)
                pe.wait_ge(dve_step, 4)
                for k in range(4):
                    last = nc.tensor.transpose(ps[:, k * P:(k + 1) * P],
                                               ends[:, k:k + 1].to_broadcast([P, P]), c.ident[:, :])
                last.then_inc(turned, 1)


def project_stage(nc, c, name, weight, source, evacuate, follow=None, columns=NODES_PAD):
    step = 512
    parts = [(a, min(step, columns - a)) for a in range(0, columns, step)]
    banks = 4
    with semaphores(nc, name + "_") as sem:
        product_ready, product_taken = sem("product_ready"), sem("product_taken")
        with nc.Block() as block:
            @block.tensor
            def _(pe):
                for k, (a, n) in enumerate(parts):
                    if k >= banks:
                        pe.wait_ge(product_taken, k - banks + 1)
                    nc.tensor.matmul(c.psum[k % banks][:, 0:n], weight, source[:, a:a + n],
                                     start=True, stop=True).then_inc(product_ready, 1)

            @block.scalar
            def _(act):
                for k, (a, n) in enumerate(parts):
                    act.wait_ge(product_ready, k + 1)
                    evacuate(slice(a, a + n), c.psum[k % banks][:, 0:n]).then_inc(product_taken, 1)

            if follow is not None:
                @block.vector
                def _(dve):
                    for k, (a, n) in enumerate(parts):
                        dve.wait_ge(product_taken, k + 1)
                        follow(slice(a, a + n))


def turn_stage(nc, c, name, source, take):
    five = 5
    with semaphores(nc, name + "_") as sem:
        turned, taken = sem("turned"), sem("taken")
        with nc.Block() as block:
            @block.tensor
            def _(pe):
                for k in range(TILES // five):
                    if k >= 2:
                        pe.wait_ge(taken, k - 1)
                    for q in range(five):
                        a = (k * five + q) * P
                        last = nc.tensor.transpose(c.psum_wide[k % 2][:, q * P:(q + 1) * P], source[:, a:a + P],
                                                   c.ident[:, :])
                    last.then_inc(turned, 1)

            @block.vector
            def _(dve):
                for k in range(TILES // five):
                    dve.wait_ge(turned, k + 1)
                    take(slice(k * five * P, (k + 1) * five * P), c.psum_wide[k % 2][:, 0:five * P]).then_inc(taken, 1)


def normalise_stage(nc, c, name, keep_x=False):
    parts = 5
    width = TILES // parts
    with semaphores(nc, name + "_") as sem:
        summed, scaled, centred, squared, spread = (sem("summed"), sem("scaled"), sem("centred"), sem("squared"), sem("spread"))
        rooted, inverted, normal, stored = sem("rooted"), sem("inverted"), sem("normal"), sem("stored")
        x3, h3, q3 = tile_view(c.x), tile_view(c.rows2), tile_view(c.rows1)
        with nc.Block() as block:
            @block.vector
            def _(dve):
                nc.vector.tensor_reduce(c.stat_a[:, :], x3, AX.X, ALU.add).then_inc(summed, 1)
                dve.wait_ge(summed, 1)
                nc.vector.tensor_scalar(c.stat_a[:, :], c.stat_a[:, :], 1.0 / D, None, ALU.mult).then_inc(scaled, 1)
                dve.wait_ge(scaled, 1)
                for k in range(parts):
                    t = slice(k * width, (k + 1) * width)
                    nc.vector.tensor_tensor(h3[:, t, :], x3[:, t, :],
                                            c.stat_a[:, t].unsqueeze(2).to_broadcast([P, width, D]),
                                            ALU.subtract).then_inc(centred, 1)
                for k in range(parts):
                    t = slice(k * width, (k + 1) * width)
                    dve.wait_ge(squared, k + 1)
                    nc.vector.tensor_reduce(c.stat_b[:, t], q3[:, t, :], AX.X, ALU.add).then_inc(spread, 1)
                dve.wait_ge(rooted, 1)
                nc.vector.reciprocal(c.stat_b[:, :], c.stat_a[:, :]).then_inc(inverted, 1)
                dve.wait_ge(inverted, 1)
                for k in range(parts):
                    t = slice(k * width, (k + 1) * width)
                    nc.vector.scalar_tensor_tensor(out=h3[:, t, :], in0=h3[:, t, :], scalar=0.0,
                                                   in1=c.stat_b[:, t].unsqueeze(2).to_broadcast([P, width, D]),
                                                   op0=ALU.max, op1=ALU.mult).then_inc(normal, 1)

            @block.scalar
            def _(act):
                for k in range(parts):
                    act.wait_ge(centred, k + 1)
                    w = slice(k * width * D, (k + 1) * width * D)
                    nc.scalar.activation(c.rows1[:, w], c.rows2[:, w], ACT.Square).then_inc(squared, 1)
                act.wait_ge(spread, parts)
                nc.scalar.activation(c.stat_a[:, :], c.stat_b[:, :], ACT.Sqrt, scale=1.0 / D,
                                     bias=c.eps_col[:, :]).then_inc(rooted, 1)

            @block.sync
            def _(sp):
                full, rest = node_rows(c.table)
                if keep_x:
                    sp.dma_start(c.x_store[:, :], c.x[:, :]).then_inc(stored, 16)
                for k in range(parts):
                    t = slice(k * width, min((k + 1) * width, FULL_TILES))
                    sp.wait_ge(normal, k + 1)
                    sp.dma_start(full[:, t, :], h3[:, t, :]).then_inc(stored, 16)
                sp.dma_start(rest, h3[0:TAIL, FULL_TILES, :]).then_inc(stored, 16)
                sp.wait_ge(stored, 16 * (parts + 1 + (1 if keep_x else 0)))


def windows_program(sp, c, rounds_done, windows_loaded, r):
    sp.wait_ge(rounds_done, r + 1)
    sp.dma_start(c.window[:, :], c.window_table[bass.ds(r, 1), :]).then_inc(windows_loaded, 16)


def attention_stage(nc, c):
    gt, h_sum = c.x, c.pair
    with semaphores(nc, "a_") as sem:
        rounds_done, windows_loaded, gate = sem("rounds_done"), sem("windows_loaded"), c.gate
        idx_loaded = [sem(f"idx_loaded{s}") for s in range(SLOTS)]
        rows_gathered = [sem(f"rows_gathered{s}") for s in range(SLOTS)]
        half_turned, half_copied, weights_summed = sem("half_turned"), sem("half_copied"), sem("weights_summed")
        denominator_added = sem("denominator_added")
        rows_turned, turned_copied, scores_ready = sem("rows_turned"), sem("turned_copied"), sem("scores_ready")
        mismatch_ready, masked, chunks_maxed = sem("mismatch_ready"), sem("masked"), sem("chunks_maxed")
        maxima_turned, maxima_found, maxima_spread = sem("maxima_turned"), sem("maxima_found"), sem("maxima_spread")
        maxima_new, maxima_step, maxima_kept, shifted = sem("maxima_new"), sem("maxima_step"), sem("maxima_kept"), sem("shifted")
        weights_ready, weighted, rescaled, added = sem("weights_ready"), sem("weighted"), sem("rescaled"), sem("added")
        replicas_cleared, cleared, iota_moved = sem("replicas_cleared"), sem("cleared"), sem("iota_moved")
        psT, psS, psM, psV = c.psum_wide[0], c.psum[4], c.psum[5], c.psum[6]
        mism, B, W = c.onehot[:, 0:512], c.onehot[:, 512:1024], c.onehot[:, 1024:1536]
        B3 = B.rearrange("p (j w) -> p j w", w=WINDOW)
        W3 = W.rearrange("p (j w) -> p j w", w=WINDOW)
        S3 = psS[:, :].rearrange("p (j w) -> p j w", w=WINDOW)
        small = c.small
        bm, mnew, mg = small[:, 0:P], small[:, P:P + WINDOW], small[:, 192:193]
        mstep = [small[:, 256 + 64 * s:320 + 64 * s] for s in range(SLOTS)]
        wsum = c.onehot[:, 1536:1536 + WINDOW]
        mscale = [small[:, 512 + 64 * s:576 + 64 * s] for s in range(SLOTS)]
        with nc.Block() as block:
            @block.sync
            def _(sp):
                rounds = sp.value_load(c.rounds_i[0:1, 0:1], min_val=1, max_val=MAX_ROUNDS)

                def body(r, g, slot, t, use, first):
                    if first:
                        windows_program(sp, c, rounds_done, windows_loaded, r)
                    sp.wait_ge(rows_turned, t + 1)
                    sp.dma_start(c.idx[:, slot, :], c.src_i[:, bass.ds(g * CHUNKS, CHUNKS)]).then_inc(idx_loaded[slot], 16)
                each_group(sp, rounds, body)

            @block.gpsimd
            def _(pool):
                rounds = pool.value_load(c.rounds_i[0:1, 0:1], min_val=1, max_val=MAX_ROUNDS)

                def body(r, g, slot, t, use, first):
                    pool.wait_ge(idx_loaded[slot], use * 16 + 16)
                    pool.wait_ge(weighted, t + 1)
                    pool.sem_inc(gate, 1)
                    for j in range(CHUNKS):
                        nc.gpsimd.indirect_dma_start(
                            c.rows[:, slot, j, :], None, c.table[:, :],
                            bass.IndirectOffsetOnAxis(ap=c.idx[:, slot, j:j + 1], axis=0)).then_inc(rows_gathered[slot], 16)
                each_group(pool, rounds, body)

            @block.tensor
            def _(pe):
                pe.sem_inc(weighted, SLOTS)
                pe.sem_inc(scores_ready, 1)
                pe.sem_inc(rows_turned, SLOTS)
                rounds = pe.value_load(c.rounds_i[0:1, 0:1], min_val=1, max_val=MAX_ROUNDS)

                def turn_maxima(t):
                    pe.wait_ge(chunks_maxed, t + 1)
                    nc.tensor.transpose(psM[:, 0:P], bm, c.ident[:, :]).then_inc(maxima_turned, 1)

                def weigh(slot, t, turn_next):
                    pe.wait_ge(weights_ready, t + 1)
                    pe.wait_ge(added, t + 1)
                    for j in range(CHUNKS):
                        if turn_next and j == CHUNKS - 3:
                            turn_maxima(t + 1)
                        last = nc.tensor.matmul(psV[:, 0:WINDOW], c.rows[:, slot, j, :], W3[:, j, :],
                                                start=(j == 0), stop=(j == CHUNKS - 1))
                    last.then_inc(weighted, 1)

                def body(r, g, slot, t, use, first):
                    if first:
                        pe.wait_ge(windows_loaded, r * 16 + 16)
                        pe.sem_inc(gate, 1)
                    pe.wait_ge(rows_gathered[slot], use * (16 * CHUNKS) + 16 * CHUNKS)
                    pe.wait_ge(turned_copied, t + 1)
                    for half, turned in enumerate((half_turned, rows_turned)):
                        for j in range(half * CHUNKS // 2, (half + 1) * CHUNKS // 2):
                            last = nc.tensor.transpose(psT[:, j * P:(j + 1) * P], c.rows[:, slot, j, :], c.ident[:, :])
                        last.then_inc(turned, 1)
                    base = pe.value_load(c.window[0:1, bass.ds(g, 1)], min_val=0, max_val=WINDOW_END)
                    pe.wait_ge(half_copied, t + 1)
                    pe.wait_ge(masked, t + 1)
                    for j in range(CHUNKS):
                        if j == CHUNKS // 2:
                            pe.wait_ge(turned_copied, t + 2)
                        last = nc.tensor.matmul(psS[:, j * WINDOW:(j + 1) * WINDOW], c.turned[:, j * P:(j + 1) * P],
                                                gt[:, bass.ds(base, WINDOW)], start=True, stop=True)
                    last.then_inc(scores_ready, 1)
                    if first:
                        turn_maxima(t)
                    else:
                        weigh((slot + SLOTS - 1) % SLOTS, t - 1, True)
                    pe.wait_ge(maxima_found, t + 1)
                    nc.tensor.transpose(psM[:, P:2 * P], mg.to_broadcast([P, P]), c.ident[:, :]).then_inc(maxima_spread, 1)

                def finish(r):
                    weigh((GROUPS - 1) % SLOTS, r * GROUPS + (GROUPS - 1), False)
                each_group(pe, rounds, body, finish)

            @block.scalar
            def _(act):
                act.sem_inc(turned_copied, 1)
                for rep in c.replicas:
                    act.dma_start(rep[:, :].rearrange("(t p) f -> p t f", p=P),
                                  c.zeros[:, :].unsqueeze(1).to_broadcast([P, TILES, D])).then_inc(replicas_cleared, 16)
                rounds = act.value_load(c.rounds_i[0:1, 0:1], min_val=1, max_val=MAX_ROUNDS)

                mid = CHUNKS * P // 2

                def copy_first_half(t):
                    act.wait_ge(half_turned, t + 1)
                    act.wait_ge(scores_ready, t + 1)
                    nc.scalar.activation(c.turned[:, 0:mid], psT[:, 0:mid], ACT.Copy).then_inc(half_copied, 1)

                def copy_second_half(t):
                    act.wait_ge(rows_turned, t + 1 + SLOTS)
                    nc.scalar.activation(c.turned[:, mid:], psT[:, mid:], ACT.Copy).then_inc(turned_copied, 1)

                def exponents(slot, t):
                    act.wait_ge(shifted, t + 1)
                    nc.scalar.activation(mscale[slot], mstep[slot], ACT.Exp)
                    act.wait_ge(weighted, t + SLOTS)
                    act.wait_ge(weights_summed, t + 1)
                    nc.scalar.activation(W, B, ACT.Exp).then_inc(weights_ready, 1)

                def body(r, g, slot, t, use, first):
                    copy_first_half(t)
                    if not first:
                        exponents((slot + SLOTS - 1) % SLOTS, t - 1)
                    copy_second_half(t)

                def finish(r):
                    exponents((GROUPS - 1) % SLOTS, r * GROUPS + (GROUPS - 1))
                each_group(act, rounds, body, finish)
                act.wait_ge(replicas_cleared, 16 * REPLICAS)

            @block.vector
            def _(dve):
                dve.sem_inc(masked, 1)
                dve.sem_inc(weights_summed, 1)
                dve.sem_inc(added, 1)
                nc.vector.memset(c.pair[:, :], 0.0).then_inc(cleared, 1)
                nc.vector.memset(c.maxima[:, :], FLOOR).then_inc(cleared, 1)
                nc.vector.tensor_copy(c.iota[:, :], c.iota0[:, :]).then_inc(cleared, 1)
                nc.vector.memset(bm, FLOOR).then_inc(cleared, 1)
                dve.wait_ge(cleared, 4)
                dve.sem_inc(rounds_done, 1)
                rounds = dve.value_load(c.rounds_i[0:1, 0:1], min_val=1, max_val=MAX_ROUNDS)
                both = c.pair[:, :].rearrange("p (k n) -> p k n", k=2)

                def sum_weights(t):
                    dve.wait_ge(weights_ready, t + 1)
                    nc.vector.tensor_reduce(wsum, W.rearrange("p (j w) -> p w j", w=WINDOW), AX.X,
                                            ALU.add).then_inc(weights_summed, 1)

                def add(g, slot, t):
                    base = dve.value_load(c.window[0:1, bass.ds(g, 1)], min_val=0, max_val=WINDOW_END)
                    dve.wait_ge(weights_summed, t + 2)
                    nc.vector.tensor_tensor(both[:, :, bass.ds(base, WINDOW)], both[:, :, bass.ds(base, WINDOW)],
                                            mscale[slot].unsqueeze(1).to_broadcast([P, 2, WINDOW]),
                                            ALU.mult).then_inc(rescaled, 1)
                    dve.wait_ge(rescaled, t + 1)
                    nc.vector.tensor_tensor(both[:, 1, bass.ds(base, WINDOW)], both[:, 1, bass.ds(base, WINDOW)],
                                            wsum, ALU.add).then_inc(denominator_added, 1)
                    dve.wait_ge(weighted, t + 1 + SLOTS)
                    nc.vector.tensor_tensor(both[:, 0, bass.ds(base, WINDOW)], both[:, 0, bass.ds(base, WINDOW)],
                                            psV[:, 0:WINDOW], ALU.add).then_inc(added, 1)
                    dve.wait_ge(denominator_added, t + 1)

                def body(r, g, slot, t, use, first):
                    if first:
                        dve.wait_ge(windows_loaded, r * 16 + 16)
                        dve.sem_inc(gate, 1)
                    nc.vector.scalar_tensor_tensor(
                        out=mism.rearrange("p (j w) -> p j w", w=WINDOW),
                        in0=c.iota[:, :].unsqueeze(1).to_broadcast([P, CHUNKS, WINDOW]),
                        scalar=c.first[:, bass.ds(g, 1)],
                        in1=c.dst[:, bass.ds(g * CHUNKS, CHUNKS)].unsqueeze(2).to_broadcast([P, CHUNKS, WINDOW]),
                        op0=ALU.add, op1=ALU.not_equal).then_inc(mismatch_ready, 1)
                    if not first:
                        sum_weights(t - 1)
                    dve.wait_ge(mismatch_ready, t + 1)
                    dve.wait_ge(scores_ready, t + 2)
                    nc.vector.scalar_tensor_tensor(out=B, in0=mism, scalar=FAR, in1=psS[:, :],
                                                   op0=ALU.mult, op1=ALU.add).then_inc(masked, 1)
                    dve.wait_ge(masked, t + 2)
                    nc.vector.tensor_reduce(bm[:, 0:WINDOW], B.rearrange("p (j w) -> p w j", w=WINDOW), AX.X,
                                            ALU.max).then_inc(chunks_maxed, 1)
                    base = dve.value_load(c.window[0:1, bass.ds(g, 1)], min_val=0, max_val=WINDOW_END)
                    dve.wait_ge(maxima_turned, t + 1)
                    nc.vector.tensor_reduce(mg, psM[:, 0:P], AX.X, ALU.max).then_inc(maxima_found, 1)
                    dve.wait_ge(maxima_spread, t + 1)
                    nc.vector.tensor_tensor(mnew, c.maxima[:, bass.ds(base, WINDOW)], psM[:, P:P + WINDOW],
                                            ALU.max).then_inc(maxima_new, 1)
                    dve.wait_ge(maxima_new, t + 1)
                    nc.vector.tensor_tensor(mstep[slot], c.maxima[:, bass.ds(base, WINDOW)], mnew,
                                            ALU.subtract).then_inc(maxima_step, 1)
                    nc.vector.tensor_tensor(B3, B3, mnew.unsqueeze(1).to_broadcast([P, CHUNKS, WINDOW]),
                                            ALU.subtract).then_inc(shifted, 1)
                    dve.wait_ge(maxima_step, t + 1)
                    nc.vector.tensor_tensor(c.maxima[:, bass.ds(base, WINDOW)], mnew, mnew,
                                            ALU.max).then_inc(maxima_kept, 1)
                    dve.wait_ge(maxima_kept, t + 1)
                    dve.sem_inc(gate, 1)
                    if not first:
                        add(g - 1, (slot + SLOTS - 1) % SLOTS, t - 1)
                        dve.wait_ge(added, t + 1)
                        dve.sem_inc(gate, 1)

                def finish(r):
                    sum_weights(r * GROUPS + (GROUPS - 1))
                    add(GROUPS - 1, (GROUPS - 1) % SLOTS, r * GROUPS + (GROUPS - 1))
                    nc.vector.tensor_scalar(c.iota[:, :], c.iota[:, :], float(WINDOW), None, ALU.add).then_inc(iota_moved, 1)
                    dve.wait_ge(iota_moved, r + 1)
                    dve.wait_ge(added, r * GROUPS + (GROUPS + 1))
                    dve.sem_inc(rounds_done, 1)
                each_group(dve, rounds, body, finish)


def sum_stage(nc, c, name, acc, edge_features=None, weighted_edges=False):
    with semaphores(nc, name + "_") as sem:
        rounds_done, windows_loaded, gate = sem("rounds_done"), sem("windows_loaded"), c.gate
        idx_loaded = [sem(f"idx_loaded{s}") for s in range(SLOTS)]
        rows_gathered = [sem(f"rows_gathered{s}") for s in range(SLOTS)]
        features_loaded = [sem(f"features_loaded{s}") for s in range(SLOTS)]
        match_ready, onehot_ready, messages_ready = sem("match_ready"), sem("onehot_ready"), sem("messages_ready")
        summed, added, iota_reset, iota_moved = sem("summed"), sem("added"), sem("iota_reset"), sem("iota_moved")
        ps = [c.psum[s] for s in range(SLOTS)]
        hot = [c.onehot[:, s * 512:(s + 1) * 512].rearrange("p (j w) -> p j w", w=WINDOW) for s in range(SLOTS)]
        rows_seen = summed if edge_features is None else messages_ready
        with nc.Block() as block:
            @block.sync
            def _(sp):
                rounds = sp.value_load(c.rounds_i[0:1, 0:1], min_val=1, max_val=MAX_ROUNDS)

                def body(r, g, slot, t, use, first):
                    if first:
                        windows_program(sp, c, rounds_done, windows_loaded, r)
                    sp.wait_ge(rows_seen, t + 1)
                    sp.dma_start(c.idx[:, slot, :], c.src_i[:, bass.ds(g * CHUNKS, CHUNKS)]).then_inc(idx_loaded[slot], 16)
                each_group(sp, rounds, body)

            if edge_features is not None:
                @block.scalar
                def _(act):
                    rounds = act.value_load(c.rounds_i[0:1, 0:1], min_val=1, max_val=MAX_ROUNDS)

                    def body(r, g, slot, t, use, first):
                        if first:
                            act.wait_ge(rounds_done, r + 1)
                            act.sem_inc(gate, 1)
                        act.wait_ge(messages_ready, t + 1)
                        if not is_last(g):
                            act.dma_start(c.features[:, slot, :, :],
                                          edge_features[bass.ds(g * GROUP, GROUP), :].rearrange("(p j) f -> p j f", j=CHUNKS)
                                          ).then_inc(features_loaded[slot], 16)
                            return
                        at, mid = FULL_GROUPS * GROUP, FULL_GROUPS * GROUP + TAIL_PARTS * CHUNKS
                        act.dma_start(c.features[0:TAIL_PARTS, slot, :, :],
                                      edge_features[at:mid, :].rearrange("(p j) f -> p j f", j=CHUNKS)
                                      ).then_inc(features_loaded[slot], 16)
                        act.dma_start(c.features[TAIL_PARTS:TAIL_PARTS + 1, slot, 0:TAIL_REST, :],
                                      edge_features[mid:EDGES, :].rearrange("(p j) f -> p j f", p=1)
                                      ).then_inc(features_loaded[slot], 16)

                    each_group(act, rounds, body)

            @block.gpsimd
            def _(pool):
                rounds = pool.value_load(c.rounds_i[0:1, 0:1], min_val=1, max_val=MAX_ROUNDS)

                def body(r, g, slot, t, use, first):
                    pool.wait_ge(idx_loaded[slot], use * 16 + 16)
                    pool.wait_ge(summed, t + 1)
                    pool.sem_inc(gate, 1)
                    for j in range(CHUNKS):
                        nc.gpsimd.indirect_dma_start(
                            c.rows[:, slot, j, :], None, c.table[:, :],
                            bass.IndirectOffsetOnAxis(ap=c.idx[:, slot, j:j + 1], axis=0)).then_inc(rows_gathered[slot], 16)
                each_group(pool, rounds, body)

            @block.tensor
            def _(pe):
                pe.sem_inc(summed, SLOTS)
                rounds = pe.value_load(c.rounds_i[0:1, 0:1], min_val=1, max_val=MAX_ROUNDS)

                def body(r, g, slot, t, use, first):
                    if edge_features is not None:
                        pe.wait_ge(messages_ready, t + 1 + SLOTS)
                    else:
                        pe.wait_ge(rows_gathered[slot], use * (16 * CHUNKS) + 16 * CHUNKS)
                    pe.wait_ge(onehot_ready, t + 1)
                    for j in range(CHUNKS):
                        last = nc.tensor.matmul(ps[slot][:, 0:WINDOW], c.rows[:, slot, j, :], hot[slot][:, j, :],
                                                start=(j == 0), stop=(j == CHUNKS - 1))
                    last.then_inc(summed, 1)
                each_group(pe, rounds, body)

            @block.vector
            def _(dve):
                dve.sem_inc(messages_ready, SLOTS)
                nc.vector.tensor_copy(c.iota[:, :], c.iota0[:, :]).then_inc(iota_reset, 1)
                if edge_features is not None:
                    nc.vector.tensor_scalar(acc, c.ht[:, :], 2.0, None, ALU.mult).then_inc(iota_reset, 1)
                else:
                    nc.vector.memset(acc, 0.0).then_inc(iota_reset, 1)
                dve.wait_ge(iota_reset, 2)
                dve.sem_inc(rounds_done, 1)
                rounds = dve.value_load(c.rounds_i[0:1, 0:1], min_val=1, max_val=MAX_ROUNDS)

                def add(g, slot, t):
                    base = dve.value_load(c.window[0:1, bass.ds(g, 1)], min_val=0, max_val=WINDOW_END)
                    dve.wait_ge(summed, t + 1 + SLOTS)
                    nc.vector.tensor_tensor(acc[:, bass.ds(base, WINDOW)], acc[:, bass.ds(base, WINDOW)],
                                            ps[slot][:, 0:WINDOW], ALU.add).then_inc(added, 1)
                    dve.wait_ge(added, t + 1)
                    dve.sem_inc(gate, 1)

                def body(r, g, slot, t, use, first):
                    if first:
                        dve.wait_ge(windows_loaded, r * 16 + 16)
                        dve.sem_inc(gate, 1)
                    made = nc.vector.scalar_tensor_tensor(
                        out=hot[slot],
                        in0=c.iota[:, :].unsqueeze(1).to_broadcast([P, CHUNKS, WINDOW]),
                        scalar=c.first[:, bass.ds(g, 1)],
                        in1=c.dst[:, bass.ds(g * CHUNKS, CHUNKS)].unsqueeze(2).to_broadcast([P, CHUNKS, WINDOW]),
                        op0=ALU.add, op1=ALU.is_equal)
                    if weighted_edges:
                        made.then_inc(match_ready, 1)
                        dve.wait_ge(match_ready, t + 1)
                        nc.vector.tensor_tensor(hot[slot], hot[slot],
                                                c.weight[:, bass.ds(g * CHUNKS, CHUNKS)].unsqueeze(2).to_broadcast([P, CHUNKS, WINDOW]),
                                                ALU.mult).then_inc(onehot_ready, 1)
                    else:
                        made.then_inc(onehot_ready, 1)
                    if edge_features is not None:
                        dve.wait_ge(rows_gathered[slot], use * (16 * CHUNKS) + 16 * CHUNKS)
                        dve.wait_ge(features_loaded[slot], use * 16 + (r * 16 if slot == (GROUPS - 1) % SLOTS else 0)
                                    + (32 if is_last(g) else 16))
                        nc.vector.tensor_tensor(c.rows[:, slot, :, :], c.rows[:, slot, :, :], c.features[:, slot, :, :],
                                                ALU.add).then_inc(messages_ready, 1)
                    if not first:
                        add(g - 1, (slot + SLOTS - 1) % SLOTS, t - 1)

                def finish(r):
                    add(GROUPS - 1, (GROUPS - 1) % SLOTS, r * GROUPS + (GROUPS - 1))
                    nc.vector.tensor_scalar(c.iota[:, :], c.iota[:, :], float(WINDOW), None, ALU.add).then_inc(iota_moved, 1)
                    dve.wait_ge(iota_moved, r + 1)
                    dve.sem_inc(rounds_done, 1)
                each_group(dve, rounds, body, finish)


def scatter_stage(nc, c):
    with semaphores(nc, "s_") as sem:
        rounds_done, windows_loaded, gate = sem("rounds_done"), sem("windows_loaded"), c.gate
        h_loaded = [sem(f"h_loaded{s}") for s in range(SLOTS)]
        PER_GROUP = 16 * (CHUNKS // REPLICAS)
        landed = [sem(f"landed{j}") for j in range(REPLICAS)]
        onehot_ready, source_ready, source_turned = sem("onehot_ready"), sem("source_ready"), sem("source_turned")
        same_ready, counts_ready, counts_copied, messages_made = sem("same_ready"), sem("counts_ready"), sem("counts_copied"), sem("messages_made")
        messages_ready, earlier_ready, earlier_counted = sem("messages_ready"), sem("earlier_ready"), sem("earlier_counted")
        detour_ready, detour_taken, rows_named = sem("detour_ready"), sem("detour_taken"), sem("rows_named")
        round_landed = sem("round_landed")
        messages_landed, iota_reset, iota_moved = sem("messages_landed"), sem("iota_reset"), sem("iota_moved")
        psR, psC, psG = c.psum_wide[0], c.psum_wide[1], c.psum_wide[2]
        hot = c.onehot[:, 0:256].bitcast(BF16)
        hot3 = hot.rearrange("p (j w) -> p j w", w=WINDOW)
        same = c.onehot[:, 256:768].bitcast(BF16)
        same3 = same.rearrange("p (j k) -> p j k", k=P)
        earlier = c.onehot[:, 768:1280].bitcast(BF16)
        earlier3 = earlier.rearrange("p (j k) -> p j k", k=P)
        hwin = c.features[:, 1, :, :]
        now, cnt, det = c.small[:, 0:8], c.small[:, 8:16], c.small[:, 16:24]
        with nc.Block() as block:
            @block.sync
            def _(sp):
                rounds = sp.value_load(c.rounds_i[0:1, 0:1], min_val=1, max_val=MAX_ROUNDS)

                def body(r, g, slot, t, use, first):
                    if first:
                        windows_program(sp, c, rounds_done, windows_loaded, r)
                        sp.wait_ge(windows_loaded, r * 16 + 16)
                        sp.sem_inc(gate, 1)
                    base = sp.value_load(c.window[0:1, bass.ds(g, 1)], min_val=0, max_val=WINDOW_END)
                    sp.wait_ge(messages_made, t + 1)
                    sp.dma_start(hwin[0:WINDOW, slot, :], c.table[bass.ds(base, WINDOW), :]).then_inc(h_loaded[slot], 16)
                each_group(sp, rounds, body)

            @block.gpsimd
            def _(pool):
                for j in range(REPLICAS):
                    pool.dma_start(c.replicas[j][NODES:NODES + P, :], c.zeros).then_inc(landed[j], 16)
                pool.sem_inc(messages_landed, SLOTS - 1)
                rounds = pool.value_load(c.rounds_i[0:1, 0:1], min_val=1, max_val=MAX_ROUNDS)

                def body(r, g, slot, t, use, first):
                    pool.wait_ge(messages_ready, t + 1)
                    pool.wait_ge(rows_named, t + 1 + SLOTS)
                    pool.sem_inc(gate, 1)
                    for j in range(CHUNKS):
                        k = j % REPLICAS
                        pool.wait_ge(landed[k], t * PER_GROUP + (j // REPLICAS + 1) * 16)
                        pool.sem_inc(gate, 1)
                        nc.gpsimd.indirect_dma_start(
                            c.replicas[k][:, :], bass.IndirectOffsetOnAxis(ap=c.idx[:, slot, j:j + 1], axis=0),
                            c.rows[:, slot, j, :], None, compute_op=ALU.add).then_inc(landed[k], 16)
                    pool.sem_inc(messages_landed, 1)
                def finish(r):
                    for j in range(REPLICAS):
                        pool.wait_ge(landed[j], r * (PER_GROUP * GROUPS) + (PER_GROUP * GROUPS + 16))
                    pool.sem_inc(round_landed, 1)
                each_group(pool, rounds, body, finish)

            @block.tensor
            def _(pe):
                pe.sem_inc(messages_made, SLOTS)
                pe.sem_inc(counts_ready, 1)
                rounds = pe.value_load(c.rounds_i[0:1, 0:1], min_val=1, max_val=MAX_ROUNDS)

                def make_messages(slot, t):
                    pe.wait_ge(counts_copied, t + 2)
                    for j in range(CHUNKS):
                        last = nc.tensor.matmul(psG[:, j * P:(j + 1) * P], c.turned[0:WINDOW, j * P:(j + 1) * P],
                                                hwin[0:WINDOW, slot, :], start=True, stop=True)
                    last.then_inc(messages_made, 1)

                def body(r, g, slot, t, use, first):
                    pe.wait_ge(source_ready, t + 1)
                    for j in range(CHUNKS):
                        last = nc.tensor.transpose(psR[:, j * P:(j + 1) * P], now[:, j:j + 1].to_broadcast([P, P]),
                                                   c.ident[:, :])
                    last.then_inc(source_turned, 1)
                    if not first:
                        make_messages((slot + SLOTS - 1) % SLOTS, t - 1)
                    pe.wait_ge(h_loaded[slot], use * 16 + 16)
                    pe.wait_ge(same_ready, t + 1)
                    pe.wait_ge(counts_copied, t + 1)
                    for j in range(CHUNKS):
                        last = nc.tensor.matmul(psC[0:WINDOW, j * P:(j + 1) * P], hot3[:, j, :], same3[:, j, :],
                                                start=True, stop=True)
                    last.then_inc(counts_ready, 1)

                def finish(r):
                    make_messages((GROUPS - 1) % SLOTS, r * GROUPS + (GROUPS - 1))
                each_group(pe, rounds, body, finish)

            @block.scalar
            def _(act):
                act.sem_inc(counts_copied, 1)
                rounds = act.value_load(c.rounds_i[0:1, 0:1], min_val=1, max_val=MAX_ROUNDS)

                def copy_messages(slot, t):
                    act.wait_ge(messages_made, t + 1 + SLOTS)
                    act.wait_ge(messages_landed, t + 1)
                    nc.scalar.activation(c.rows[:, slot, :, :].rearrange("p j f -> p (j f)"), psG[:, :],
                                         ACT.Copy).then_inc(messages_ready, 1)

                def copy_counts(t):
                    act.wait_ge(counts_ready, t + 2)
                    act.wait_ge(messages_made, t + SLOTS)
                    nc.scalar.activation(c.turned[0:WINDOW, :], psC[0:WINDOW, :], ACT.Copy).then_inc(counts_copied, 1)

                def body(r, g, slot, t, use, first):
                    if not first:
                        copy_messages((slot + SLOTS - 1) % SLOTS, t - 1)
                    copy_counts(t)

                def finish(r):
                    copy_messages((GROUPS - 1) % SLOTS, r * GROUPS + (GROUPS - 1))
                each_group(act, rounds, body, finish)

            @block.vector
            def _(dve):
                dve.sem_inc(rows_named, SLOTS)
                nc.vector.tensor_copy(c.iota[:, :], c.iota0[:, :]).then_inc(iota_reset, 1)
                dve.wait_ge(iota_reset, 1)
                dve.sem_inc(rounds_done, 1)
                rounds = dve.value_load(c.rounds_i[0:1, 0:1], min_val=1, max_val=MAX_ROUNDS)

                def body(r, g, slot, t, use, first):
                    nc.vector.tensor_copy(now, c.src_i[:, bass.ds(g * CHUNKS, CHUNKS)]).then_inc(source_ready, 1)
                    dve.wait_ge(counts_ready, t + 1)
                    nc.vector.scalar_tensor_tensor(
                        out=hot3,
                        in0=c.iota[:, :].unsqueeze(1).to_broadcast([P, CHUNKS, WINDOW]),
                        scalar=c.first[:, bass.ds(g, 1)],
                        in1=c.dst[:, bass.ds(g * CHUNKS, CHUNKS)].unsqueeze(2).to_broadcast([P, CHUNKS, WINDOW]),
                        op0=ALU.add, op1=ALU.is_equal).then_inc(onehot_ready, 1)
                    dve.wait_ge(source_ready, t + 1)
                    dve.wait_ge(source_turned, t + 1)
                    nc.vector.tensor_tensor(same3, psR[:, :].rearrange("p (j k) -> p j k", k=P),
                                            now.unsqueeze(2).to_broadcast([P, CHUNKS, P]),
                                            ALU.is_equal).then_inc(same_ready, 1)
                    dve.wait_ge(same_ready, t + 1)
                    nc.vector.tensor_tensor(earlier3, same3, c.before[:, :].unsqueeze(1).to_broadcast([P, CHUNKS, P]),
                                            ALU.mult).then_inc(earlier_ready, 1)
                    nc.vector.tensor_scalar(det, now, -1.0, c.dump[:, :], ALU.mult, ALU.add).then_inc(detour_ready, 1)
                    dve.wait_ge(earlier_ready, t + 1)
                    nc.vector.tensor_reduce(cnt, earlier3, AX.X, ALU.add).then_inc(earlier_counted, 1)
                    dve.wait_ge(detour_ready, t + 1)
                    dve.wait_ge(earlier_counted, t + 1)
                    nc.vector.scalar_tensor_tensor(out=det, in0=cnt, scalar=1.0, in1=det, op0=ALU.min,
                                                   op1=ALU.mult).then_inc(detour_taken, 1)
                    dve.wait_ge(detour_taken, t + 1)
                    dve.wait_ge(messages_landed, t + 1)
                    nc.vector.tensor_tensor(c.idx[:, slot, :], det, now, ALU.add).then_inc(rows_named, 1)
                    dve.wait_ge(rows_named, t + 1 + SLOTS)
                    dve.sem_inc(gate, 1)

                def finish(r):
                    nc.vector.tensor_scalar(c.iota[:, :], c.iota[:, :], float(WINDOW), None, ALU.add).then_inc(iota_moved, 1)
                    dve.wait_ge(iota_moved, r + 1)
                    dve.wait_ge(messages_made, r * GROUPS + (GROUPS + SLOTS))
                    dve.wait_ge(round_landed, r + 1)
                    dve.sem_inc(rounds_done, 1)
                each_group(dve, rounds, body, finish)


def divide_stage(nc, c):
    num, den = c.pair[:, 0:NODES_PAD], c.pair[:, NODES_PAD:]
    step, banks = 512, 4
    parts = [(a, min(step, NODES_PAD - a)) for a in range(0, NODES_PAD, step)]
    with semaphores(nc, "divide_") as sem:
        share_summed, guarded, inverted, divided, x_back = (sem("share_summed"), sem("guarded"), sem("inverted"),
                                                            sem("divided"), sem("x_back"))
        with nc.Block() as block:
            @block.tensor
            def _(pe):
                for k, (a, n) in enumerate(parts):
                    if k >= banks:
                        pe.wait_ge(guarded, k - banks + 1)
                    nc.tensor.matmul(c.psum[k % banks][:, 0:n], c.ones[:, :], den[:, a:a + n],
                                     start=True, stop=True).then_inc(share_summed, 1)

            @block.vector
            def _(dve):
                for k, (a, n) in enumerate(parts):
                    dve.wait_ge(share_summed, k + 1)
                    nc.vector.tensor_scalar(den[:, a:a + n], c.psum[k % banks][:, 0:n], 1e-30, None,
                                            ALU.max).then_inc(guarded, 1)
                dve.wait_ge(guarded, len(parts))
                nc.vector.reciprocal(den, den).then_inc(inverted, 1)
                dve.wait_ge(inverted, 1)
                nc.vector.tensor_tensor(num, num, den, ALU.mult).then_inc(divided, 1)

            @block.sync
            def _(sp):
                sp.dma_start(c.x[:, :], c.x_store[:, :]).then_inc(x_back, 16)
                sp.wait_ge(x_back, 16)


def gather_replicas_stage(nc, c):
    halves = [c.pair[:, 0:NODES_PAD], c.pair[:, NODES_PAD:]]
    with semaphores(nc, "replicas_") as sem:
        loaded = [sem(f"loaded{k}") for k in range(2)]
        summed, first_loaded = sem("summed"), sem("first_loaded")
        rows = [rep[:, :].rearrange("(t p) f -> p t f", p=P) for rep in c.replicas]
        with nc.Block() as block:
            @block.sync
            def _(sp):
                sp.dma_start(tile_view(c.rows2), rows[0]).then_inc(first_loaded, 16)
                for k in range(1, REPLICAS):
                    if k >= 3:
                        sp.wait_ge(summed, k - 2)
                    sp.dma_start(halves[k % 2].rearrange("p (t f) -> p t f", f=D), rows[k]).then_inc(loaded[k % 2], 16)

            @block.vector
            def _(dve):
                dve.wait_ge(first_loaded, 16)
                for k in range(1, REPLICAS):
                    dve.wait_ge(loaded[k % 2], 16 * ((k + 1) // 2))
                    nc.vector.tensor_tensor(c.rows2[:, :], c.rows2[:, :], halves[k % 2], ALU.add).then_inc(summed, 1)
                    dve.wait_ge(summed, k)


def one_plus_eps_stage(nc, c):
    with semaphores(nc, "eps_") as sem:
        spread, made = sem("spread"), sem("made")
        with nc.Block() as block:
            @block.tensor
            def _(pe):
                nc.tensor.matmul(c.psum[0][:, 0:1], c.ones[0:1, :], c.eps_one[:, :], start=True, stop=True).then_inc(spread, 1)

            @block.vector
            def _(dve):
                nc.vector.memset(c.eps_col[:, :], LN_EPS).then_inc(made, 1)
                dve.wait_ge(spread, 1)
                nc.vector.tensor_scalar(c.eps_plus[:, :], c.psum[0][:, 0:1], 1.0, None, ALU.add).then_inc(made, 1)
                dve.wait_ge(made, 2)


def batchnorm_stage(nc, c, name, buf, gamma, beta):
    pieces = 25
    width = NODES // pieces
    stats = c.turned[:, 0:6 * pieces]
    mv, root, scale, shift = c.turned[:, 160:162], c.turned[:, 162:163], c.turned[:, 163:164], c.turned[:, 164:165]
    inv = c.turned[:, 165:166]
    with semaphores(nc, name + "_") as sem:
        piece_done, aggregated, rooted, scaled, applied, step = (sem("piece_done"), sem("aggregated"), sem("rooted"),
                                                                sem("scaled"), sem("applied"), sem("step"))
        with nc.Block() as block:
            @block.vector
            def _(dve):
                for k in range(pieces):
                    nc.vector.bn_stats(stats[:, 6 * k:6 * k + 6], buf[:, k * width:(k + 1) * width]).then_inc(piece_done, 1)
                dve.wait_ge(piece_done, pieces)
                nc.vector.bn_aggr(mv, stats).then_inc(aggregated, 1)
                dve.wait_ge(rooted, 1)
                nc.vector.reciprocal(inv, root).then_inc(step, 1)
                dve.wait_ge(step, 1)
                nc.vector.tensor_tensor(scale, inv, gamma, ALU.mult).then_inc(step, 1)
                dve.wait_ge(step, 2)
                nc.vector.tensor_tensor(shift, mv[:, 0:1], scale, ALU.mult).then_inc(step, 1)
                dve.wait_ge(step, 3)
                nc.vector.tensor_tensor(shift, beta, shift, ALU.subtract).then_inc(scaled, 1)

            @block.scalar
            def _(act):
                act.wait_ge(aggregated, 1)
                nc.scalar.activation(root, mv[:, 1:2], ACT.Sqrt, bias=c.eps_col[:, :]).then_inc(rooted, 1)
                act.wait_ge(scaled, 1)
                nc.scalar.activation(buf, buf, ACT.Relu, scale=scale, bias=shift).then_inc(applied, 1)
                act.wait_ge(applied, 1)


def store_stage(nc, c, out):
    with semaphores(nc) as sem:
        stored = sem("out_stored")
        with nc.Block() as block:
            @block.sync
            def _(sp):
                full, rest = node_rows(out)
                sp.dma_start(full, tile_view(c.x)[:, 0:FULL_TILES, :]).then_inc(stored, 16)
                sp.dma_start(rest, tile_view(c.x)[0:TAIL, FULL_TILES, :]).then_inc(stored, 16)
                sp.wait_ge(stored, 32)


def gnn_program(nc, io, out):
    c = Core()
    with ExitStack() as ctx:
        sb = lambda n, shape, dt=F32: ctx.enter_context(nc.sbuf_tensor(n, shape, dt))
        c.gate = ctx.enter_context(nc.semaphore("gate"))
        c.x = sb("x_rows", [P, NODES_PAD])
        c.ht = sb("h_columns", [P, NODES_PAD])
        c.pair = sb("pair", [P, 2 * NODES_PAD])
        c.maxima = sb("maxima", [P, NODES_PAD])
        c.rows1 = c.pair[:, NODES_PAD:]
        c.rows2 = c.maxima
        c.temp = c.ht
        c.src_i = sb("src_i", [P, GROUPS * CHUNKS], I32)
        c.dst = sb("dst", [P, GROUPS * CHUNKS])
        c.weight = sb("edge_w", [P, GROUPS * CHUNKS])
        c.first = sb("first_dst", [P, GROUPS])
        c.window = sb("window", [1, GROUPS], I32)
        c.rounds_i = sb("rounds_i", [P, 1], I32)
        c.rows = sb("gathered_rows", [P, SLOTS, CHUNKS, D])
        c.features = sb("edge_features", [P, SLOTS, CHUNKS, D])
        c.turned = c.features[:, 0, :, :].rearrange("p j f -> p (j f)")
        c.onehot = sb("onehot", [P, SLOTS * CHUNKS * WINDOW])
        c.idx = sb("idx", [P, SLOTS, CHUNKS], I32)
        c.small = sb("small", [P, 768])
        c.ident = sb("ident", [P, P])
        c.ones = sb("ones", [P, P])
        c.zeros2 = sb("zeros", [P, 2 * D])
        c.zeros = c.zeros2[:, 0:D]
        c.before = sb("before", [P, P])
        c.iota0 = sb("iota0", [P, WINDOW])
        c.iota = sb("iota", [P, WINDOW])
        c.dump = sb("dump", [P, 1])
        c.stat_a = sb("stat_a", [P, TILES])
        c.stat_b = sb("stat_b", [P, TILES])
        c.eps_col = sb("eps_col", [P, 1])
        c.eps_plus = sb("eps_plus", [P, 1])
        c.eps_one = sb("eps_one", [1, 1])
        c.weight_names = ["L0_gnn_Wq", "L0_gnn_Wk", "L0_gnn_Wv", "L0_gnn_Wo", "L1_gnn_W1", "L1_gnn_W2",
                          "L2_gnn_w1", "L2_gnn_w2"]
        c.column_names = ["L1_gnn_b1", "L1_gnn_b2", "L2_gnn_b1", "L2_gnn_gamma1", "L2_gnn_beta1",
                          "L2_gnn_b2", "L2_gnn_gamma2", "L2_gnn_beta2"]
        c.mats = sb("mats", [P, len(c.weight_names), D])
        c.cols = sb("cols", [P, len(c.column_names)])
        c.setup_loads = 3 + 1 + len(c.weight_names) + len(c.column_names) + 1 + 1
        ps = ctx.enter_context(nc.psum_tensor("ps", [P, 8, 512], F32))
        c.psum = [ps[:, k, :] for k in range(8)]
        flat = ps[:, :, :].rearrange("p b n -> p (b n)")
        c.psum_wide = [flat[:, 1024 * k:1024 * (k + 1)] for k in range(4)]
        c.table = nc.dram_tensor("h_table", (NODES_PAD, D), F32).ap()
        c.x_store = nc.dram_tensor("x_store", (P, NODES_PAD), F32).ap()
        c.window_table = nc.dram_tensor("window_table", (MAX_ROUNDS, GROUPS), I32).ap()
        c.replicas = [nc.dram_tensor(f"replica{j}", (NODES_PAD, D), F32).ap() for j in range(REPLICAS)]
        mat = lambda n: c.mats[:, c.weight_names.index(n), :]
        col = lambda n: c.cols[:, c.column_names.index(n):c.column_names.index(n) + 1]
        ht, num, acc2 = c.ht, c.pair[:, 0:NODES_PAD], c.pair[:, NODES_PAD:]
        add_to_x = lambda cols, p: nc.vector.tensor_tensor(c.x[:, cols], c.x[:, cols], p, ALU.add)
        to_ht = lambda cols, p: nc.vector.tensor_copy(ht[:, cols], p)

        setup_stage(nc, c, io)
        one_plus_eps_stage(nc, c)

        normalise_stage(nc, c, "n0", keep_x=True)
        turn_stage(nc, c, "t0", c.rows2, to_ht)
        wkt = c.small[:, 0:P]
        with semaphores(nc) as sem:
            wk_turned, wk_copied = sem("wk_turned"), sem("wk_copied")
            with nc.Block() as block:
                @block.tensor
                def _(pe):
                    nc.tensor.transpose(c.psum[0][:, 0:P], mat("L0_gnn_Wk"), c.ident[:, :]).then_inc(wk_turned, 1)

                @block.vector
                def _(dve):
                    dve.wait_ge(wk_turned, 1)
                    nc.vector.tensor_copy(wkt, c.psum[0][:, 0:P]).then_inc(wk_copied, 1)
                    dve.wait_ge(wk_copied, 1)
        project_stage(nc, c, "q", mat("L0_gnn_Wq"), ht, lambda s, p: nc.scalar.activation(num[:, s], p, ACT.Copy))
        project_stage(nc, c, "g", wkt, num,
                      lambda s, p: nc.scalar.activation(c.x[:, s], p, ACT.Copy, scale=float(D) ** -0.5))
        attention_stage(nc, c)
        divide_stage(nc, c)
        project_stage(nc, c, "v", mat("L0_gnn_Wv"), num, lambda s, p: nc.scalar.activation(acc2[:, s], p, ACT.Copy))
        project_stage(nc, c, "o", mat("L0_gnn_Wo"), acc2, lambda s, p: nc.scalar.activation(num[:, s], p, ACT.Copy),
                      follow=lambda s: nc.vector.tensor_tensor(num[:, s], num[:, s], ht[:, s], ALU.add))
        turn_stage(nc, c, "b0", num, add_to_x)

        normalise_stage(nc, c, "n1")
        turn_stage(nc, c, "t1", c.rows2, to_ht)
        sum_stage(nc, c, "m1", num, edge_features=io["edge_attr_128"])
        project_stage(nc, c, "p1", mat("L1_gnn_W1"), num,
                      lambda s, p: nc.scalar.activation(acc2[:, s], p, ACT.Identity, bias=col("L1_gnn_b1")),
                      follow=lambda s: nc.vector.scalar_tensor_tensor(out=acc2[:, s], in0=acc2[:, s], scalar=0.01,
                                                                      in1=acc2[:, s], op0=ALU.mult, op1=ALU.max))
        project_stage(nc, c, "p2", mat("L1_gnn_W2"), acc2,
                      lambda s, p: nc.scalar.activation(num[:, s], p, ACT.Identity, bias=col("L1_gnn_b2")))
        turn_stage(nc, c, "b1", num, add_to_x)

        normalise_stage(nc, c, "n2")
        turn_stage(nc, c, "t2", c.rows2, to_ht)
        scatter_stage(nc, c)
        gather_replicas_stage(nc, c)
        turn_stage(nc, c, "a2", c.rows2,
                   lambda cols, p: nc.vector.scalar_tensor_tensor(out=num[:, cols], in0=ht[:, cols],
                                                                  scalar=c.eps_plus[:, :], in1=p,
                                                                  op0=ALU.mult, op1=ALU.add))
        project_stage(nc, c, "p3", mat("L2_gnn_w1"), num,
                      lambda s, p: nc.scalar.activation(acc2[:, s], p, ACT.Identity, bias=col("L2_gnn_b1")))
        batchnorm_stage(nc, c, "bn1", acc2, col("L2_gnn_gamma1"), col("L2_gnn_beta1"))
        project_stage(nc, c, "p4", mat("L2_gnn_w2"), acc2,
                      lambda s, p: nc.scalar.activation(num[:, s], p, ACT.Identity, bias=col("L2_gnn_b2")))
        batchnorm_stage(nc, c, "bn2", num, col("L2_gnn_gamma2"), col("L2_gnn_beta2"))
        turn_stage(nc, c, "b2", num, add_to_x)

        normalise_stage(nc, c, "n3")
        sum_stage(nc, c, "m3", num, weighted_edges=True)
        turn_stage(nc, c, "b3", num, add_to_x)
        store_stage(nc, c, out)


_INS = ["x", "src", "dst", "edge_attr_128", "edge_weight", "L0_gnn_Wq", "L0_gnn_Wk", "L0_gnn_Wv", "L0_gnn_Wo",
        "L1_gnn_W1", "L1_gnn_b1", "L1_gnn_W2", "L1_gnn_b2", "L2_gnn_eps", "L2_gnn_w1", "L2_gnn_b1",
        "L2_gnn_gamma1", "L2_gnn_beta1", "L2_gnn_w2", "L2_gnn_b2", "L2_gnn_gamma2", "L2_gnn_beta2"]


def kernel(**inputs):
    import numpy as _np
    import concourse.bacc as _bacc
    from concourse import mybir as _mybir
    from concourse.bass_utils import run_bass_kernel_spmd as _run

    nc = _bacc.Bacc("TRN2", target_bir_lowering=False, num_devices=1)
    arrays, io = {}, {}
    for name in _INS:
        a = _np.ascontiguousarray(inputs[name])
        arrays[f"in_{name}_dram"] = a
        io[name] = nc.dram_tensor(f"in_{name}_dram", a.shape, _mybir.dt.from_np(a.dtype), kind="ExternalInput").ap()
    out = nc.dram_tensor("out_dram", (NODES, D), _mybir.dt.float32, kind="ExternalOutput").ap()
    gnn_program(nc, io, out)
    r = _run(nc, [arrays], core_ids=[0])
    return r.results[0]["out_dram"]
```
